# Optimizing a Trainium2 kernel written in Bass

```python
import numpy as np
import jax
import jax.numpy as jnp

def _softmax(x, axis=-1):
    return jax.nn.softmax(x, axis=axis)
def _gelu(x):
    return jax.nn.gelu(x, approximate=True)
def _silu(x):
    return jax.nn.silu(x)
def _sigmoid(x):
    return jax.nn.sigmoid(x)
def _layernorm(x, axis=-1, eps=1e-5):
    m = jnp.mean(x, axis=axis, keepdims=True)
    v = jnp.var(x, axis=axis, keepdims=True)
    return (x - m) / jnp.sqrt(v + eps)
def _scatter_add(tgt, idx, src, axis=0):
    return tgt.at[idx].add(src)
def _segment_sum(src, seg, n):
    return jax.ops.segment_sum(src, seg, n)

kernel_name = 'mk_conv_preact_d2_conv_nchw384_3040aa'

def setup_inputs(seed: int = 0):
    np.random.seed(seed)
    _w = jnp.asarray
    def _rec_inputs():
        import jax
        import jax.numpy as jnp
        _gk = jax.random.key(seed)
        x = -0.0001836 + 1 * jax.random.normal(jax.random.fold_in(_gk, 1), (8, 384, 128, 128), jnp.float32)
        return x
    x = _rec_inputs()
    def _L0_conv_setup():
        import jax, jax.numpy as jnp
        import numpy as np
        from jax import lax
        C = 384
        key = jax.random.key(seed)
        k1, k2 = jax.random.split(key)
        x = jax.random.normal(k1, (16, C, 128, 128), dtype=jnp.float32)
        k = jax.random.normal(k2, (C, 1, 3, 3), dtype=jnp.float32)
        return {'x': x, 'k': k}
    _L0_conv_all = _L0_conv_setup()
    _L0_conv_in = {k: v for k, v in _L0_conv_all.items() if k in ('k', )}
    del _L0_conv_all

    def _L1_conv_setup():
        import jax, jax.numpy as jnp
        import numpy as np
        EPS = 1e-05

        def _dwconv(x, w, pad):
            return jax.lax.conv_general_dilated(x, w, window_strides=(1, 1), padding=[(pad, pad), (pad, pad)], feature_group_count=w.shape[0], dimension_numbers=('NCHW', 'OIHW', 'NCHW'))

        def _bn(y, g, b, m, v):
            scale = (g / jnp.sqrt(v + EPS))[None, :, None, None]
            shift = (b - m * g / jnp.sqrt(v + EPS))[None, :, None, None]
            return y * scale + shift
        key = jax.random.key(seed)
        ks = jax.random.split(key, 16)
        C, KL, KS = (384, 13, 3)
        N, H, W = (16, 64, 64)
        inp = {'x': jax.random.normal(ks[0], (N, C, H, W), jnp.float32), 'w_large': jax.random.normal(ks[1], (C, 1, KL, KL), jnp.float32) * 0.05, 'w_small': jax.random.normal(ks[2], (C, 1, KS, KS), jnp.float32) * 0.2, 'g_l': jax.random.normal(ks[3], (C,), jnp.float32), 'b_l': jax.random.normal(ks[4], (C,), jnp.float32), 'm_l': jax.random.normal(ks[5], (C,), jnp.float32), 'v_l': jax.random.uniform(ks[6], (C,), jnp.float32, 0.5, 1.5), 'g_s': jax.random.normal(ks[7], (C,), jnp.float32), 'b_s': jax.random.normal(ks[8], (C,), jnp.float32), 'm_s': jax.random.normal(ks[9], (C,), jnp.float32), 'v_s': jax.random.uniform(ks[10], (C,), jnp.float32, 0.5, 1.5), 'g_i': jax.random.normal(ks[11], (C,), jnp.float32), 'b_i': jax.random.normal(ks[12], (C,), jnp.float32), 'm_i': jax.random.normal(ks[13], (C,), jnp.float32), 'v_i': jax.random.uniform(ks[14], (C,), jnp.float32, 0.5, 1.5)}
        return inp
    _L1_conv_all = _L1_conv_setup()
    _L1_conv_in = {k: v for k, v in _L1_conv_all.items() if k in ('w_large', 'w_small', 'g_l', 'b_l', 'm_l', 'v_l', 'g_s', 'b_s', 'm_s', 'v_s', 'g_i', 'b_i', 'm_i', 'v_i', )}
    del _L1_conv_all

    return {
        "x": x,
        "L0_conv_k": _L0_conv_in["k"],
        "L1_conv_w_large": _L1_conv_in["w_large"],
        "L1_conv_w_small": _L1_conv_in["w_small"],
        "L1_conv_g_l": _L1_conv_in["g_l"],
        "L1_conv_b_l": _L1_conv_in["b_l"],
        "L1_conv_m_l": _L1_conv_in["m_l"],
        "L1_conv_v_l": _L1_conv_in["v_l"],
        "L1_conv_g_s": _L1_conv_in["g_s"],
        "L1_conv_b_s": _L1_conv_in["b_s"],
        "L1_conv_m_s": _L1_conv_in["m_s"],
        "L1_conv_v_s": _L1_conv_in["v_s"],
        "L1_conv_g_i": _L1_conv_in["g_i"],
        "L1_conv_b_i": _L1_conv_in["b_i"],
        "L1_conv_m_i": _L1_conv_in["m_i"],
        "L1_conv_v_i": _L1_conv_in["v_i"],
    }

def reference(x, L0_conv_k, L1_conv_w_large, L1_conv_w_small, L1_conv_g_l, L1_conv_b_l, L1_conv_m_l, L1_conv_v_l, L1_conv_g_s, L1_conv_b_s, L1_conv_m_s, L1_conv_v_s, L1_conv_g_i, L1_conv_b_i, L1_conv_m_i, L1_conv_v_i):
    import jax
    import jax.numpy as jnp
    def _L0_conv_ref(x, k):
        import jax, jax.numpy as jnp
        import numpy as np
        from jax import lax
        C = 384
        return lax.conv_general_dilated(x, k, window_strides=(1, 1), padding=((1, 1), (1, 1)), rhs_dilation=(1, 1), dimension_numbers=('NCHW', 'OIHW', 'NCHW'), feature_group_count=C)

    def _L1_conv_ref(x, w_large, w_small, g_l, b_l, m_l, v_l, g_s, b_s, m_s, v_s, g_i, b_i, m_i, v_i):
        import jax, jax.numpy as jnp
        import numpy as np
        EPS = 1e-05

        def _dwconv(x, w, pad):
            return jax.lax.conv_general_dilated(x, w, window_strides=(1, 1), padding=[(pad, pad), (pad, pad)], feature_group_count=w.shape[0], dimension_numbers=('NCHW', 'OIHW', 'NCHW'))

        def _bn(y, g, b, m, v):
            scale = (g / jnp.sqrt(v + EPS))[None, :, None, None]
            shift = (b - m * g / jnp.sqrt(v + EPS))[None, :, None, None]
            return y * scale + shift
        kl = w_large.shape[-1]
        ks = w_small.shape[-1]
        out = _bn(_dwconv(x, w_large, kl // 2), g_l, b_l, m_l, v_l) + _bn(_dwconv(x, w_small, ks // 2), g_s, b_s, m_s, v_s) + _bn(x, g_i, b_i, m_i, v_i)
        return out

    def _gn(v, G=32, eps=1e-5):
        B_, C_, H_, W_ = v.shape
        g = v.reshape(B_, G, C_ // G, H_, W_)
        m = jnp.mean(g, axis=(2, 3, 4), keepdims=True)
        s = jnp.var(g, axis=(2, 3, 4), keepdims=True)
        return ((g - m) / jnp.sqrt(s + eps)).reshape(v.shape)

    def _ln_c(v, eps=1e-6):
        m = jnp.mean(v, axis=1, keepdims=True)
        s = jnp.var(v, axis=1, keepdims=True)
        return (v - m) / jnp.sqrt(s + eps)

    def _ln_t(v, eps=1e-5):
        m = jnp.mean(v, axis=-1, keepdims=True)
        s = jnp.var(v, axis=-1, keepdims=True)
        return (v - m) / jnp.sqrt(s + eps)

    def _to_tokens(v):
        B_, C_, H_, W_ = v.shape
        return v.reshape(B_, C_, H_ * W_).transpose(0, 2, 1)
    def _from_tokens(t, like):
        B_, C_, H_, W_ = like.shape
        return t.transpose(0, 2, 1).reshape(B_, C_, H_, W_)

    x = x + _L0_conv_ref(_gn(x), L0_conv_k)
    x = x + _L1_conv_ref(_gn(x), L1_conv_w_large, L1_conv_w_small, L1_conv_g_l, L1_conv_b_l, L1_conv_m_l, L1_conv_v_l, L1_conv_g_s, L1_conv_b_s, L1_conv_m_s, L1_conv_v_s, L1_conv_g_i, L1_conv_b_i, L1_conv_m_i, L1_conv_v_i)
    return x


_drawn_inputs = setup_inputs


def setup_inputs(seed=0):
    import zlib

    import numpy as np

    out = dict(_drawn_inputs(seed))
    spreads = {}
    factors = {}
    for name, (base, spread) in spreads.items():
        noise = np.random.default_rng([zlib.crc32(name.encode()), seed]).standard_normal(out[name].shape)
        drawn = base * np.exp(spread * noise) if base else spread * noise
        out[name] = jnp.asarray(drawn.astype(out[name].dtype))
    for name, factor in factors.items():
        out[name] = (out[name] * factor).astype(out[name].dtype)
    return out
```

```python
from contextlib import ExitStack

import concourse.bass as bass
from concourse import mybir

F32 = mybir.dt.float32
F16 = mybir.dt.float16
U32 = mybir.dt.uint32
ALU = mybir.AluOpType
ACT = mybir.ActivationFunctionType
AX = mybir.AxisListType

P = 128
GC = 12
UI = 4
BC = 3
Q = GC // BC
SLOTS = 4
NBI = BC * UI
K0, K1 = 3, 13
R1 = K1 // 2
BW = 4
BH = P // BW
NBLK = P // BH
WIN = 4
HW_ = 8
HWIN = 2
HROWS = 2 * R1
KH = HW_ * HROWS
UP = P // BW + WIN
W0P = P + 2
RUN = 2 * NBI * UP
PADT = K1 - 1 + 2 * (BW - 1) + 1
NORM_SCALE = 128.0
FILTER_SCALE = 4096.0
EPS = 1e-5
PARTS = [(0, 0), (0, 1), (1, 0)]

R1N = (BH + 2 * R1) * BW * 2 * WIN
RHN = (BH + 4 * R1) * BW * 2 * HWIN
R0N = W0P * 2 * K0

L_CONV1 = 5
L_EVAC = 6
L_FINAL = 7
L_NORM1 = 3


def preact_convs(nc, x, k0, w_large, w_small, params, out, tab0, tab1, tabh, tabs, mat0, mat1, math):
    N, C = x.shape[0], x.shape[1]
    NG = C // GC
    HALVES = N // UI
    NU = NG * HALVES
    NT = NU * Q
    PC = min(P, C)
    KC = C // PC
    assert HALVES == 2 and NU >= 5

    with ExitStack() as ctx:
        def sb(name, shape, dt):
            return ctx.enter_context(nc.sbuf_tensor(name, shape, dt))

        def sem(name):
            return ctx.enter_context(nc.semaphore(name))

        xs = sb("xs", [P, SLOTS, GC, UI, P], F32)
        g0 = sb("g0", [P, NBI, P], F32)
        g1 = sb("g1", [P, NBI, P], F32)
        n0 = sb("n0", [P, 2, 2, NBI, W0P], F16)
        n1 = sb("n1", [P, BW, 2, NBI, UP], F16)
        blk = sb("blk", [P, 2, NBLK, 2, NBI, UP], F16)
        halo = sb("halo", [KH, 2, NBLK, 2, NBI, UP], F16)
        ysum = sb("ysum", [P, NBLK, NBI * (P // BW)], F32)
        yrow = sb("yrow", [P, BW, NBI, P // BW], F32)
        WSN = BH * BW * 2 * WIN
        wblk = sb("wblk", [P, 2 * BC, WSN], F16)
        WHN = BH * BW * 2 * HWIN
        whalo = sb("whalo", [KH, 2 * BC, WHN], F16)
        W0N = P * 2 * K0
        w0 = sb("w0", [P, BC, W0N], F16)
        scales = sb("scales", [P, C, 3], F32)
        sc0 = sb("sc0", [P, 2, BC], F32)
        sc1 = sb("sc1", [P, 2, BC, 2], F32)
        ones = sb("ones", [P, P], F32)
        mhalf = sb("mhalf", [P, 9], F32)
        st = [sb("st0", [P, UI, 3, 6], F32), sb("st1", [P, UI, Q, 6], F32)]
        NS = 10
        nrm = [sb(f"nrm{k}", [P, NS, UI], F32) for k in range(2)]

        ps0 = [ctx.enter_context(nc.psum_tensor(f"ps0_{j}", [P, 512], F32)) for j in range(BC)]
        ps1 = [ctx.enter_context(nc.psum_tensor(f"ps1_{j}", [P, 512], F32)) for j in range(BC)]
        psn = ctx.enter_context(nc.psum_tensor("psn", [P, 512], F32))

        WL = K1 * K1
        prep = xs[:, SLOTS - 1].rearrange("p c i w -> p (c i w)")
        at = [0]

        def scratch(n, dt=F32):
            words = n if dt == F32 else (n + 1) // 2
            v = prep[0:PC, at[0]:at[0] + words]
            at[0] += words
            return v if dt == F32 else v.bitcast(dt)

        p_wl = scratch(KC * WL).rearrange("p (k n) -> p k n", k=KC)
        p_ws = scratch(KC * 9).rearrange("p (k n) -> p k n", k=KC)
        p_k0 = scratch(KC * 9).rearrange("p (k n) -> p k n", k=KC)
        p_par = scratch(12 * KC).rearrange("p (b r k) -> p b r k", b=3, r=4)
        p_bn = scratch(4 * 3 * KC).rearrange("p (r b k) -> p r b k", r=4, b=3)
        p_sm = scratch(16 * KC).rearrange("p (r k) -> p r k", k=KC)
        p_w = scratch(KC * WL).rearrange("p (k n) -> p k n", k=KC)
        p_lo = scratch(KC * WL).rearrange("p (k n) -> p k n", k=KC)
        p_pad = [scratch(KC * K1 * PADT + 1, F16)[:, 0:KC * K1 * PADT] for _ in range(2)]
        p_pad = [v.rearrange("p (k d c) -> p k d c", k=KC, d=K1) for v in p_pad]
        T1N = BW * K1 * BW * 2 * WIN
        THN = HW_ * K1 * BW * 2 * HWIN
        T0N = K0 * 2 * K0
        p_zero = prep[:, at[0]:at[0] + R1N // 2].bitcast(F16)
        at[0] += R1N // 2
        p_t1 = blk[0:PC].rearrange("p r k a n u -> p (r k a n u)")[:, 0:KC * T1N].rearrange("p (k n) -> p k n", k=KC)
        p_th = scratch(KC * THN, F16).rearrange("p (k n) -> p k n", k=KC)
        p_t0 = scratch(KC * T0N, F16).rearrange("p (k n) -> p k n", k=KC)
        p_sc = scratch(3 * KC).rearrange("p (k r) -> p k r", r=3)
        assert at[0] <= GC * UI * P

        s_par = sem("params_loaded")
        s_prep = sem("prep_step")
        s_veps = sem("prep_var_ready")
        s_rstd = sem("prep_rstd_ready")
        s_tab = sem("tables_stored")
        s_scl = sem("scales_loaded")
        s_zero = sem("buffers_zeroed")
        s_held = sem("waits_held")
        s_ld = [sem(f"x_loaded_{k}") for k in range(UI)]
        s_w0 = sem("w0_loaded")
        s_w1 = [sem(f"w1_loaded_{r}") for r in range(2)]
        s_m0 = [sem(f"matrices0_laid_{r}") for r in range(2)]
        s_m1 = [sem(f"matrices1_laid_{r}") for r in range(2)]
        s_c0 = [sem(f"conv0_done_{j}") for j in range(BC)]
        s_c1 = [sem(f"conv1_done_{j}") for j in range(BC)]
        s_g0, s_h0, s_l0 = sem("norm0_done"), sem("high0_done"), sem("low0_done")
        s_g1, s_h1, s_l1 = sem("norm1_done"), sem("high1_done"), sem("low1_done")
        s_x1 = sem("layer0_summed")
        s_b1 = sem("stats1_taken")
        s_b0 = sem("stats0_taken")
        s_sc0, s_sc1 = sem("scales0_copied"), sem("scales1_copied")
        s_rg = [sem(f"regrouped_{r}") for r in range(2)]
        s_ev = sem("sums_evacuated")
        s_yr = sem("sums_regrouped")
        s_fin = sem("layer1_summed")
        s_st = sem("stored")
        names = ["aggregated", "mean_summed", "mean_off", "mean_off_squared", "var_part", "var_summed",
                 "var_copied", "rstd_powered", "norm_scale", "norm_shift"]
        s_n = [{n: sem(f"{n}_{k}") for n in names} for k in range(2)]
        N_TAB = 16 * 10
        N_RG = NBLK + 2 * 2 * (NBLK - 1)

        block = ctx.enter_context(nc.Block())

        def wait(eng, s, value):
            if not isinstance(value, int) or value > 0:
                eng.wait_ge(s, value)

        def hold(eng, s, value):
            wait(eng, s, value)
            if not isinstance(value, int):
                eng.sem_inc(s_held, 1)

        def schedule(eng, tick):
            for t in range(-5, 2 * Q):
                tick(t // Q, t % Q)
            with eng.Fori(2, NU - 2) as U:
                for q in range(Q):
                    tick(U, q)
            for t in range((NU - 2) * Q, NT + L_FINAL):
                tick(t // Q, t % Q)

        def back(U, q, lag):
            return U + (q - lag) // Q, (q - lag) % Q

        def live(U):
            return not isinstance(U, int) or 0 <= U < NU

        def chan(U, q):
            return (U // HALVES) * GC + q * BC

        def batch_no(U, q):
            return U * Q + q

        def slot(U):
            return xs[:, U % SLOTS]

        def ring(count_per, U, q):
            return (U * (Q // 2) + q // 2 + 1) * count_per

        def high_low(part, lo):
            v0 = 2 - lo
            return n1[:, 2 * lo:2 * lo + 2, part, :, v0:v0 + P // BW].rearrange("p j n v -> p n j v")

        @block.sync
        def _(sp):
            src = {"wl": (p_wl, w_large.rearrange("(k p) o a b -> p k (o a b)", p=PC)),
                   "ws": (p_ws, w_small.rearrange("(k p) o a b -> p k (o a b)", p=PC)),
                   "k0": (p_k0, k0.rearrange("(k p) o a b -> p k (o a b)", p=PC))}
            for dst, a in src.values():
                sp.dma_start(dst, a).then_inc(s_par, 16)
            with nc.allow_non_contiguous_dma(reason="one value per channel"):
                for b in range(3):
                    for r in range(4):
                        sp.dma_start(p_par[:, b, r, :],
                                     params[b][r].rearrange("(k p) -> p k", p=PC)).then_inc(s_par, 16)

            def load(U, q):
                V = U + 2
                if q != 3 or not live(V):
                    return
                hold(sp, s_st, (V - SLOTS + 1) * Q * BC * 16)
                if isinstance(V, int) and V == SLOTS - 1:
                    sp.wait_ge(s_tab, N_TAB)
                for k in range(UI):
                    hold(sp, s_ld[k], V * 16)
                    sp.dma_start(slot(V)[:, :, k, :],
                                 x[(V % HALVES) * UI + k, bass.ds((V // HALVES) * GC, GC)].rearrange("c h w -> h c w")
                                 ).then_inc(s_ld[k], 16)

            def regroup_sums(U, q):
                V, r = back(U, q, L_EVAC)
                if not live(V):
                    return
                b = batch_no(V, r)
                hold(sp, s_ev, b + 1)
                hold(sp, s_fin, b)
                p = ysum[:].ap[0][0]
                for k in range(NBLK):
                    sp.dma_start(yrow[BH * k:BH * (k + 1)].rearrange("p j n u -> p j (n u)"),
                                 ysum[:, k, :]).then_inc(s_yr, 16)

            def regroup_norm(U, q):
                V, r = back(U, q, L_NORM1)
                if not live(V):
                    return
                b = batch_no(V, r)
                if isinstance(b, int) and b == 0:
                    sp.wait_ge(s_tab, N_TAB)
                hold(sp, s_l1, b + 1)
                hold(sp, s_c1[BC - 1], b - 1)
                flat = n1[:].rearrange("p j a n u -> p j (a n u)")
                for k in range(NBLK):
                    sp.dma_start(blk[:, r % 2, k].rearrange("p a n u -> p (a n u)"), flat[BH * k:BH * (k + 1)])\
                        .then_inc(s_rg[r % 2], 16)
                for side in range(2):
                    for k in range(1 - side, NBLK - side):
                        row = BH * k - R1 if side == 0 else BH * (k + 1)
                        for a in range(2):
                            sp.dma_start(halo[2 * a + side::4, r % 2, k].rearrange("p a n u -> p (a n u)")[:, 0:RUN - a],
                                         flat[row:row + R1, :, a:RUN]).then_inc(s_rg[r % 2], 16)

            def store(U, q):
                V, r = back(U, q, L_FINAL)
                if not live(V):
                    return
                hold(sp, s_fin, batch_no(V, r) + 1)
                for j in range(BC):
                    sp.dma_start(out[bass.ds((V % HALVES) * UI, UI), chan(V, r) + j].rearrange("i h w -> h i w"),
                                 slot(V)[:, r * BC + j]).then_inc(s_st, 16)

            sp.wait_ge(s_zero, 3)

            def tick(U, q):
                load(U, q)
                regroup_sums(U, q)
                store(U, q)
                regroup_norm(U, q)

            schedule(sp, tick)
            sp.wait_ge(s_st, NT * BC * 16)

        @block.gpsimd
        def _(pool):
            nc.gpsimd.memset(mhalf[:], -0.5).then_inc(s_zero, 1)
            nc.gpsimd.memset(halo[:], 0.0).then_inc(s_zero, 1)
            pool.wait_ge(s_zero, 2)
            pool.wait_ge(s_veps, 1)
            nc.gpsimd.tensor_tensor(p_bn[:, 1].rearrange("p b k -> p (b k)"), p_bn[:, 0].rearrange("p b k -> p (b k)"),
                                    mhalf[0:PC, 0:3 * KC], ALU.pow).then_inc(s_rstd, 1)
            pool.wait_ge(s_prep, PREP_STEPS)
            kp = "(k p) n -> p k n"
            for t, v in ((tab1, p_t1), (tabh, p_th), (tab0, p_t0), (tabs, p_sc)):
                pool.dma_start(t.rearrange(kp, p=PC), v).then_inc(s_tab, 16)
            for t in (mat1, math, mat0):
                for r in range(2):
                    v = t[r].rearrange("c p n -> p c n")
                    n, width = v.shape[0], v.shape[2]
                    pool.dma_start(v, p_zero[0:n, 0:width].unsqueeze(1).to_broadcast([n, BC, width])).then_inc(s_tab, 16)
            pool.wait_ge(s_tab, N_TAB)
            pool.dma_start(scales[:].rearrange("p c r -> p (c r)"),
                           tabs.rearrange("(o c) r -> o (c r)", o=1).to_broadcast([P, C * 3])).then_inc(s_scl, 16)

            def spread_bands(mat, r, c, tab, channel, first, cols, apart, rows, step, done):
                row = mat.shape[3]
                run = tab.shape[1] // cols
                dst, src = mat[r % 2, c], tab[bass.ds(channel, 1)]
                pool.dma_start(bass.AP(tensor=dst.tensor, offset=dst.offset + first,
                                       ap=[[apart * row, cols], [cols * apart * row + step, rows], [1, run]]),
                               bass.AP(tensor=src.tensor, offset=src.offset, ap=[[run, cols], [0, rows], [1, run]])
                               ).then_inc(done, 16)

            def lay0(U, q):
                V, r = back(U, q, -2)
                if not live(V):
                    return
                hold(pool, s_w0, (batch_no(V, r) - 1) * 16)
                src, dst = tab0[bass.ds(chan(V, r), BC)], mat0[r % 2]
                pool.dma_start(bass.AP(tensor=dst.tensor, offset=dst.offset,
                                       ap=[[P * R0N, BC], [R0N + 2 * K0, P], [1, T0N]]),
                               bass.AP(tensor=src.tensor, offset=src.offset, ap=[[T0N, BC], [0, P], [1, T0N]])
                               ).then_inc(s_m0[r % 2], 16)

            def load_w0(U, q):
                V, r = back(U, q, -1)
                if not live(V):
                    return
                b = batch_no(V, r)
                hold(pool, s_m0[r % 2], ring(16, V, r))
                hold(pool, s_c0[BC - 1], b)
                pool.dma_start(w0[:], mat0[r % 2, :, :, 2 * K0:2 * K0 + W0N].rearrange("c p n -> p c n"))\
                    .then_inc(s_w0, 16)

            def lay1(U, q):
                V, r = back(U, q, L_CONV1 - 2)
                if not live(V):
                    return
                b = batch_no(V, r)
                hold(pool, s_w1[r % 2], ring(32, V, r) - 32)
                for c in range(BC):
                    spread_bands(mat1, r, c, tab1, chan(V, r) + c, 0, BW, 1, BH, BW * 2 * WIN, s_m1[r % 2])
                    for side in range(2):
                        step = BW * 2 * HWIN
                        first = side * (RHN + (BH + R1) * step)
                        spread_bands(math, r, c, tabh, chan(V, r) + c, first, HW_, 2, R1, step, s_m1[r % 2])

            def load_w1(U, q):
                V, r = back(U, q, L_CONV1 - 1)
                if not live(V):
                    return
                b = batch_no(V, r)
                hold(pool, s_m1[r % 2], ring(16 * 3 * BC, V, r))
                hold(pool, s_c1[BC - 1], b - 1)
                at1, ath = R1 * BW * 2 * WIN, HROWS * BW * 2 * HWIN
                c = (r % 2) * BC
                pool.dma_start(wblk[:, c:c + BC], mat1[r % 2, :, :, at1:at1 + WSN].rearrange("c p n -> p c n"))\
                    .then_inc(s_w1[r % 2], 16)
                pool.dma_start(whalo[:, c:c + BC], math[r % 2, :, :, ath:ath + WHN].rearrange("c p n -> p c n"))\
                    .then_inc(s_w1[r % 2], 16)

            def power(U, q, k):
                V = U + 1 if k == 0 else U
                if q != (2 if k == 0 else 3) or not live(V):
                    return
                pool.wait_ge(s_n[k]["var_copied"], V + 1)
                nc.gpsimd.tensor_tensor(nrm[k][:, 6], nrm[k][:, 5], mhalf[:, 0:UI], ALU.pow)\
                    .then_inc(s_n[k]["rstd_powered"], 1)

            def tick(U, q):
                lay1(U, q)
                lay0(U, q)
                load_w1(U, q)
                power(U, q, 0)
                load_w0(U, q)
                power(U, q, 1)

            schedule(pool, tick)

        @block.scalar
        def _(act):
            def evacuate(U, q):
                V, r = back(U, q, L_EVAC)
                if not live(V):
                    return
                b = batch_no(V, r)
                wait(act, s_yr, b * NBLK * 16)
                act.wait_ge(s_sc1, b + 1)
                for j in range(BC):
                    act.wait_ge(s_c1[j], b + 1)
                    ins = nc.scalar.activation(
                        ysum[:].rearrange("p k (c n) -> p k c n", c=BC)[:, :, j],
                        ps1[j][:].rearrange("p (k n) -> p k n", k=NBLK), ACT.Identity,
                        scale=sc1[:, r % 2, j, 0:1], bias=sc1[:, r % 2, j, 1:2])
                ins.then_inc(s_ev, 1)

            def norm(U, q, k, g):
                gv = g[:].rearrange("p (c i) w -> p c i w", c=BC)
                for i in range(UI):
                    ins = nc.scalar.activation(gv[:, :, i], slot(U)[:, q * BC:(q + 1) * BC, i], ACT.Identity,
                                               scale=nrm[k][:, 7, i:i + 1], bias=nrm[k][:, 8, i:i + 1])
                return ins

            def norm0(U, q):
                V, r = back(U, q, -1)
                if not live(V):
                    return
                b = batch_no(V, r)
                act.wait_ge(s_n[0]["norm_shift"], V + 1)
                wait(act, s_l0, b)
                norm(V, r, 0, g0).then_inc(s_g0, 1)
                act.wait_ge(s_g0, b + 1)
                wait(act, s_c0[BC - 1], b - 1)
                nc.scalar.activation(n0[:, r % 2, 0, :, 1:P + 1], g0[:], ACT.Copy).then_inc(s_h0, 1)

            def norm1(U, q):
                V, r = back(U, q, L_NORM1)
                if not live(V):
                    return
                b = batch_no(V, r)
                act.wait_ge(s_n[1]["norm_shift"], V + 1)
                wait(act, s_l1, b)
                norm(V, r, 1, g1).then_inc(s_g1, 1)
                act.wait_ge(s_g1, b + 1)
                if not isinstance(b, int) or b > 0:
                    pV, pr = back(V, r, 1)
                    act.wait_ge(s_rg[pr % 2], ring(16 * N_RG, pV, pr))
                gv = g1[:].rearrange("p n (v j) -> p n j v", j=BW)
                for lo in range(2):
                    ins = nc.scalar.activation(high_low(0, lo), gv[:, :, 2 - 2 * lo:4 - 2 * lo], ACT.Copy)
                ins.then_inc(s_h1, 1)

            act.wait_ge(s_zero, 3)

            def tick(U, q):
                evacuate(U, q)
                norm0(U, q)
                norm1(U, q)

            schedule(act, tick)

        @block.vector
        def _(dve):
            step = [0]

            def link(ins):
                ins.then_inc(s_prep, 1)
                step[0] += 1
                dve.wait_ge(s_prep, step[0])

            nc.vector.memset(n1[:], 0.0)
            nc.vector.memset(ones[:], 1.0 / P)
            nc.vector.memset(n0[:], 0.0).then_inc(s_zero, 1)
            dve.wait_ge(s_par, 15 * 16)
            nc.vector.tensor_scalar(p_bn[:, 0], p_par[:, :, 3], EPS, None, ALU.add).then_inc(s_veps, 1)
            dve.wait_ge(s_rstd, 1)
            link(nc.vector.tensor_tensor(p_bn[:, 2], p_par[:, :, 0], p_bn[:, 1], ALU.mult))
            link(nc.vector.tensor_tensor(p_bn[:, 3], p_par[:, :, 2], p_bn[:, 2], ALU.mult))
            link(nc.vector.tensor_tensor(p_bn[:, 3], p_par[:, :, 1], p_bn[:, 3], ALU.subtract))
            link(nc.vector.tensor_tensor(p_sm[:, 0], p_bn[:, 3, 0], p_bn[:, 3, 1], ALU.add))
            link(nc.vector.tensor_tensor(p_sc[:, :, 2], p_sm[:, 0], p_bn[:, 3, 2], ALU.add))

            def per_chunk(v, n):
                return v.unsqueeze(2).to_broadcast([PC, KC, n])

            link(nc.vector.tensor_tensor(p_w[:], p_wl[:], per_chunk(p_bn[:, 2, 0], WL), ALU.mult))
            link(nc.vector.tensor_tensor(p_ws[:], p_ws[:], per_chunk(p_bn[:, 2, 1], 9), ALU.mult))
            w2 = p_w.rearrange("p k (a b) -> p k a b", a=K1)
            c = K1 // 2
            link(nc.vector.tensor_tensor(w2[:, :, c - 1:c + 2, c - 1:c + 2], w2[:, :, c - 1:c + 2, c - 1:c + 2],
                                         p_ws.rearrange("p k (a b) -> p k a b", a=3), ALU.add))
            link(nc.vector.tensor_tensor(w2[:, :, c, c], w2[:, :, c, c], p_bn[:, 2, 2], ALU.add))

            def power_of_two(w, at_, s):
                mx, mn, pw, inv = (p_sm[:, at_ + i] for i in range(4))
                nc.vector.tensor_reduce(mx, w, AX.X, ALU.max)
                link(nc.vector.tensor_reduce(mn, w, AX.X, ALU.min))
                link(nc.vector.tensor_scalar(mn, mn, -1.0, 2.0 ** -100, ALU.mult, ALU.max))
                link(nc.vector.tensor_tensor(mx, mx, mn, ALU.max))
                link(nc.vector.tensor_scalar(pw.bitcast(U32), mx.bitcast(U32), 0x7F800000, None, ALU.bitwise_and))
                link(nc.vector.reciprocal(inv, pw))
                link(nc.vector.tensor_scalar(inv, inv, FILTER_SCALE, None, ALU.mult))
                link(nc.vector.tensor_scalar(s, pw, 1.0 / (FILTER_SCALE * NORM_SCALE), None, ALU.mult))
                return inv

            inv1 = power_of_two(p_w, 1, p_sc[:, :, 1])
            link(nc.vector.tensor_tensor(p_w[:], p_w[:], per_chunk(inv1, WL), ALU.mult))
            nc.vector.memset(p_pad[0], 0.0)
            nc.vector.memset(p_zero, 0.0)
            link(nc.vector.memset(p_pad[1], 0.0))
            pads = [v[:, :, :, BW - 1:BW - 1 + K1] for v in p_pad]
            link(nc.vector.tensor_copy(pads[0], w2))
            link(nc.vector.tensor_tensor(p_lo.rearrange("p k (a b) -> p k a b", a=K1), w2, pads[0], ALU.subtract))
            link(nc.vector.tensor_copy(pads[1], p_lo.rearrange("p k (a b) -> p k a b", a=K1)))
            for table, cols, wins, width in ((p_t1, BW, WIN, BW), (p_th, HW_, HWIN, HW_)):
                tv = table.rearrange("p k (j d o a w) -> p k j d o a w", j=cols, d=K1, o=BW, a=2)
                for j in range(cols):
                    at_j = j if cols == BW else 2 * (j % BW) + j // BW
                    for o in range(BW):
                        for a in range(2):
                            f = p_pad[a][:, :, K1 - 1, j - o + BW - 1:j - o + BW]
                            rev = bass.AP(tensor=f.tensor, offset=f.offset,
                                          ap=[f.ap[0], [K1 * PADT, KC], [-PADT, K1], [width, wins]])
                            ins = nc.vector.tensor_copy(tv[:, :, at_j, :, o, a, :], rev)
            link(ins)
            inv0 = power_of_two(p_k0, 6, p_sc[:, :, 0])
            link(nc.vector.tensor_tensor(p_k0[:], p_k0[:], per_chunk(inv0, 9), ALU.mult))
            t0 = p_t0.rearrange("p k (d a w) -> p k d a w", d=K0, a=2)
            for d in range(K0):
                ins = nc.vector.tensor_copy(t0[:, :, d, 0], p_k0[:, :, (K0 - 1 - d) * K0:(K0 - d) * K0])
            link(ins)
            for d in range(K0):
                ins = nc.vector.tensor_tensor(t0[:, :, d, 1], p_k0[:, :, (K0 - 1 - d) * K0:(K0 - d) * K0],
                                              t0[:, :, d, 0], ALU.subtract)
            link(ins)
            assert step[0] == PREP_STEPS, step[0]
            dve.wait_ge(s_scl, 16)

            def final(U, q):
                V, r = back(U, q, L_FINAL)
                if not live(V):
                    return
                b = batch_no(V, r)
                dve.wait_ge(s_yr, (b + 1) * NBLK * 16)
                dve.wait_ge(s_x1, b + 1)
                xv = slot(V)[:, r * BC:(r + 1) * BC].rearrange("p c i (u j) -> p (c i) j u", j=BW)
                nc.vector.tensor_tensor(xv, xv, yrow[:].rearrange("p j n u -> p n j u"), ALU.add).then_inc(s_fin, 1)

            def copy_scales(U, q):
                if live(U):
                    b = batch_no(U, q)
                    nc.vector.tensor_copy(sc0[:, q % 2], scales[:, bass.ds(chan(U, q), BC), 0]).then_inc(s_sc0, 1)
                V, r = back(U, q, L_EVAC - 1)
                if live(V):
                    b = batch_no(V, r)
                    wait(dve, s_ev, b - 1)
                    nc.vector.tensor_copy(sc1[:, r % 2], scales[:, bass.ds(chan(V, r), BC), 1:3]).then_inc(s_sc1, 1)

            def sum0(U, q):
                if not live(U):
                    return
                b = batch_no(U, q)
                dve.wait_ge(s_sc0, b + 1)
                for j in range(BC):
                    dve.wait_ge(s_c0[j], b + 1)
                    xv = slot(U)[:, q * BC + j].rearrange("p i w -> p (i w)")
                    ins = nc.vector.scalar_tensor_tensor(out=xv, in0=ps0[j][:], scalar=sc0[:, q % 2, j:j + 1],
                                                         in1=xv, op0=ALU.mult, op1=ALU.add)
                ins.then_inc(s_x1, 1)
                hold(dve, s_x1, b + 1)
                for i in range(UI):
                    ins = nc.vector.bn_stats(st[1][:, i, q], slot(U)[:, q * BC:(q + 1) * BC, i])
                ins.then_inc(s_b1, 1)

            def stats0(U, q):
                V = U + 1
                if q > 1 or not live(V):
                    return
                for i in (2 * q, 2 * q + 1):
                    hold(dve, s_ld[i], (V + 1) * 16)
                    for c in range(3):
                        ins = nc.vector.bn_stats(st[0][:, i, c], slot(V)[:, c * 4:(c + 1) * 4, i])
                ins.then_inc(s_b0, 1)

            def finish_norm(k, V):
                s, n = s_n[k], nrm[k]
                mv = n[:, 0:2].rearrange("p a i -> p i a")
                for i in range(UI):
                    ins = nc.vector.bn_aggr(mv[:, i], st[k][:, i].rearrange("p a s -> p (a s)"))
                ins.then_inc(s["aggregated"], 1)
                dve.wait_ge(s["aggregated"], V + 1)
                dve.wait_ge(s["mean_summed"], V + 1)
                off = 8 * k
                nc.vector.tensor_copy(n[:, 9], psn[:, off:off + UI])
                nc.vector.tensor_tensor(n[:, 2], n[:, 0], psn[:, off:off + UI], ALU.subtract)\
                    .then_inc(s["mean_off"], 1)
                dve.wait_ge(s["mean_off"], V + 1)
                nc.vector.tensor_tensor(n[:, 3], n[:, 2], n[:, 2], ALU.mult).then_inc(s["mean_off_squared"], 1)
                dve.wait_ge(s["mean_off_squared"], V + 1)
                nc.vector.tensor_tensor(n[:, 4], n[:, 3], n[:, 1], ALU.add).then_inc(s["var_part"], 1)

            def finish_norm2(k, V):
                s, n = s_n[k], nrm[k]
                dve.wait_ge(s["var_summed"], V + 1)
                off = 8 * k + UI
                nc.vector.tensor_scalar(n[:, 5], psn[:, off:off + UI], EPS, None, ALU.add).then_inc(s["var_copied"], 1)

            def finish_norm3(k, V):
                s, n = s_n[k], nrm[k]
                dve.wait_ge(s["rstd_powered"], V + 1)
                wait(dve, s_g0 if k == 0 else s_g1, V * Q)
                nc.vector.tensor_scalar(n[:, 7], n[:, 6], NORM_SCALE, None, ALU.mult).then_inc(s["norm_scale"], 1)
                dve.wait_ge(s["norm_scale"], V + 1)
                nc.vector.scalar_tensor_tensor(out=n[:, 8], in0=n[:, 9], scalar=-1.0, in1=n[:, 7],
                                               op0=ALU.mult, op1=ALU.mult).then_inc(s["norm_shift"], 1)

            def low0(U, q):
                V, r = back(U, q, -1)
                if not live(V):
                    return
                dve.wait_ge(s_h0, batch_no(V, r) + 1)
                nc.vector.tensor_tensor(n0[:, r % 2, 1, :, 1:P + 1], g0[:], n0[:, r % 2, 0, :, 1:P + 1],
                                        ALU.subtract).then_inc(s_l0, 1)

            def low1(U, q):
                V, r = back(U, q, L_NORM1)
                if not live(V):
                    return
                dve.wait_ge(s_h1, batch_no(V, r) + 1)
                gv = g1[:].rearrange("p n (v j) -> p n j v", j=BW)
                for lo in range(2):
                    ins = nc.vector.tensor_tensor(high_low(1, lo), gv[:, :, 2 - 2 * lo:4 - 2 * lo],
                                                  high_low(0, lo), ALU.subtract)
                ins.then_inc(s_l1, 1)

            def tick(U, q):
                fin0 = q == 2 and live(U + 1)
                fin1 = q == 3 and live(U)
                copy_scales(U, q)
                if fin0:
                    hold(dve, s_b0, 2 * (U + 2))
                    finish_norm(0, U + 1)
                sum0(U, q)
                if fin0:
                    finish_norm2(0, U + 1)
                if fin1:
                    hold(dve, s_b1, batch_no(U, q) + 1)
                    finish_norm(1, U)
                low0(U, q)
                if fin0:
                    finish_norm3(0, U + 1)
                if fin1:
                    finish_norm2(1, U)
                final(U, q)
                if fin1:
                    finish_norm3(1, U)
                stats0(U, q)
                low1(U, q)

            schedule(dve, tick)

        @block.tensor
        def _(pe):
            def matrix(w, step, first):
                return w.rearrange("p (m n) -> p n m", n=step)[:, first]

            def conv0(U, q):
                if not live(U):
                    return
                b = batch_no(U, q)
                pe.wait_ge(s_w0, (b + 1) * 16)
                pe.wait_ge(s_l0, b + 1)
                wait(pe, s_x1, b)
                for j in range(BC):
                    n = 0
                    for wp, xp in PARTS:
                        for d in range(K0):
                            lhs = matrix(w0[:, j], 2 * K0, wp * K0 + d)
                            rhs = n0[:, q % 2, xp, j * UI:(j + 1) * UI, d:d + P]
                            ins = nc.tensor.matmul(ps0[j][:].rearrange("p (i w) -> p i w", i=UI), lhs, rhs,
                                                   start=n == 0, stop=n == 3 * K0 - 1)
                            n += 1
                    ins.then_inc(s_c0[j], 1)

            def average(k, V, part):
                s = s_n[k]
                off = 8 * k + UI * part
                if part == 0:
                    pe.wait_ge(s["aggregated"], V + 1)
                    rhs, done = nrm[k][:, 0], s["mean_summed"]
                else:
                    pe.wait_ge(s["var_part"], V + 1)
                    rhs, done = nrm[k][:, 4], s["var_summed"]
                nc.tensor.matmul(psn[:, off:off + UI], ones[:], rhs, start=True, stop=True).then_inc(done, 1)

            def conv1_products(j, r):
                todo = []
                for wp, xp in PARTS:
                    for a in range(WIN):
                        lhs = matrix(wblk[:, (r % 2) * BC + j], 2 * WIN, wp * WIN + a)
                        todo.append((lhs, blk[:, r % 2, :, xp, j * UI:(j + 1) * UI, a:a + P // BW]))
                for wp, xp in PARTS:
                    for a in range(HWIN):
                        lhs = matrix(whalo[:, (r % 2) * BC + j], 2 * HWIN, wp * HWIN + a)
                        todo.append((lhs, halo[:, r % 2, :, xp, j * UI:(j + 1) * UI, 2 * a:2 * a + P // BW]))
                return todo

            def tick(U, q):
                V, r = back(U, q, L_CONV1)
                fin0 = q == 2 and live(U + 1)
                fin1 = q == 3 and live(U)
                if fin0:
                    average(0, U + 1, 0)
                conv0(U, q)
                if fin0:
                    average(0, U + 1, 1)
                if not live(V):
                    if fin1:
                        average(1, U, 0)
                        average(1, U, 1)
                    return
                b = batch_no(V, r)
                for j in range(BC):
                    if j == 0:
                        pe.wait_ge(s_w1[r % 2], ring(32, V, r))
                        pe.wait_ge(s_rg[r % 2], ring(16 * N_RG, V, r))
                        wait(pe, s_ev, b)
                    todo = conv1_products(j, r)
                    for n, (lhs, rhs) in enumerate(todo):
                        if fin1 and j == 1 and n in (0, 9):
                            average(1, U, n // 9)
                        ins = nc.tensor.matmul(ps1[j][:].rearrange("p (k i u) -> p k i u", k=NBLK, i=UI), lhs, rhs,
                                               start=n == 0, stop=n == len(todo) - 1)
                    ins.then_inc(s_c1[j], 1)

            pe.wait_ge(s_zero, 3)
            schedule(pe, tick)


PREP_STEPS = 9 + 7 + 5 + 1 + 7 + 3

_PARAMS = [[f"L1_conv_{p}_{b}" for p in "gbmv"] for b in "lsi"]
_INS = ["x", "L0_conv_k", "L1_conv_w_large", "L1_conv_w_small"] + [n for row in _PARAMS for n in row]


def kernel(**inputs):
    import numpy as _np
    import concourse.bacc as _bacc
    from concourse import mybir as _mybir
    from concourse.bass_utils import run_bass_kernel_spmd as _run

    nc = _bacc.Bacc("TRN2", target_bir_lowering=False, num_devices=1)
    arrays, args = {}, {}
    for name in _INS:
        a = _np.ascontiguousarray(inputs[name])
        arrays[f"in_{name}_dram"] = a
        args[name] = nc.dram_tensor(f"in_{name}_dram", a.shape, _mybir.dt.from_np(a.dtype), kind="ExternalInput").ap()
    shape = inputs["x"].shape
    C = shape[1]
    out = nc.dram_tensor("out_0_dram", shape, _mybir.dt.float32, kind="ExternalOutput").ap()
    f16 = _mybir.dt.float16
    tab0 = nc.dram_tensor("tab0", (C, K0 * 2 * K0), f16, kind="Internal").ap()
    tab1 = nc.dram_tensor("tab1", (C, BW * K1 * BW * 2 * WIN), f16, kind="Internal").ap()
    tabh = nc.dram_tensor("tabh", (C, HW_ * K1 * BW * 2 * HWIN), f16, kind="Internal").ap()
    tabs = nc.dram_tensor("tabs", (C, 3), _mybir.dt.float32, kind="Internal").ap()
    mat0 = nc.dram_tensor("mat0", (2, BC, P, R0N), f16, kind="Internal").ap()
    mat1 = nc.dram_tensor("mat1", (2, BC, P, R1N), f16, kind="Internal").ap()
    math = nc.dram_tensor("math", (2, BC, KH, RHN), f16, kind="Internal").ap()
    preact_convs(nc, args["x"], args["L0_conv_k"], args["L1_conv_w_large"], args["L1_conv_w_small"],
                 [[args[n] for n in row] for row in _PARAMS], out, tab0, tab1, tabh, tabs, mat0, mat1, math)
    r = _run(nc, [arrays], core_ids=[0])
    return r.results[0]["out_0_dram"]
```

```python
from contextlib import ExitStack

import concourse.bass as bass
from concourse import mybir

F32 = mybir.dt.float32
F16 = mybir.dt.float16
U32 = mybir.dt.uint32
ALU = mybir.AluOpType
ACT = mybir.ActivationFunctionType
AX = mybir.AxisListType

P = 128
GC = 12
UI = 4
HALVES = 2
BC = 3
Q = GC // BC
SLOTS = 4
NBI = BC * UI
K0, K1 = 3, 13
R1 = K1 // 2
BW = 4
BH = P // BW
NBLK = P // BH
WIN = 4
HC = WIN * BW
KH = R1 * HC
UP = P // BW + WIN - 1
W0P = P + 2
RUN = 2 * NBI * UP
PADT = K1 - 1 + 2 * (BW - 1) + 1
NORM_SCALE = 128.0
FILTER_SCALE = 4096.0
EPS = 1e-5
PARTS = [(0, 0), (0, 1), (1, 0)]

R1N = (BH + 2 * R1) * BW * 2 * WIN
RHN = (BH + 4 * R1) * BW * 2
R0N = W0P * 2 * K0

L_CONV1 = 5
L_EVAC = 6
L_FINAL = 7
L_NORM1 = 3
L_HALO = 4
LAY_AHEAD = 6


class Unit:

    def __init__(self, group, n):
        self.group, self.n = group, n

    def __add__(self, k):
        return Unit(self.group, self.n + k)

    @property
    def known(self):
        return isinstance(self.group, int)

    @property
    def number(self):
        return self.group * HALVES + self.n

    @property
    def half(self):
        return self.n % HALVES

    @property
    def group_no(self):
        return self.group + self.n // HALVES


def preact_convs(nc, x, k0, w_large, w_small, params, out, tab0, tab1, tabh, tabs, mat0, mat1, math):
    N, C = x.shape[0], x.shape[1]
    NG = C // GC
    NU = NG * HALVES
    NT = NU * Q
    PC = min(P, C)
    KC = C // PC
    assert N == HALVES * UI and NG >= 3

    with ExitStack() as ctx:
        def sb(name, shape, dt):
            return ctx.enter_context(nc.sbuf_tensor(name, shape, dt))

        def sem(name):
            return ctx.enter_context(nc.semaphore(name))

        xs = sb("xs", [P, SLOTS, GC, UI, P], F32)
        g0 = sb("g0", [P, NBI, P], F32)
        g1 = sb("g1", [P, NBI, P], F32)
        n0 = sb("n0", [P, 2, NBI, W0P], F16)
        n1 = sb("n1", [P, BW, 2, NBI, UP], F16)
        blk = sb("blk", [P, 2, NBLK, 2, NBI, UP], F16)
        halo = sb("halo", [KH, 2, 2, NBLK - 1, 2, NBI, UP], F16)
        ysum = sb("ysum", [P, NBLK, NBI * (P // BW)], F32)
        yrow = sb("yrow", [P, BW, NBI, P // BW], F32)
        WSN = BH * BW * 2 * WIN
        wblk = sb("wblk", [P, GC, WSN], F16)
        WHN = BH * BW * 2
        whalo = sb("whalo", [KH, GC, 2, WHN], F16)
        W0N = P * 2 * K0
        w0 = sb("w0", [P, BC, W0N], F16)
        scales = sb("scales", [P, 2, GC * 3], F32)
        ones = sb("ones", [P, P], F32)
        st = [sb(f"st{k}", [P, UI, Q, 6], F32) for k in range(2)]
        NS = 8
        sizes = [NS * UI, NS * UI, 2 * BC, 2 * BC * 2, UI]
        small = sb("small", [P, sum(sizes)], F32)
        views = [small[:, sum(sizes[:i]):sum(sizes[:i + 1])] for i in range(len(sizes))]
        nrm = [v.rearrange("p (s i) -> p s i", s=NS) for v in views[0:2]]
        sc0 = views[2].rearrange("p (h c) -> p h c", h=2)
        sc1 = views[3].rearrange("p (h c r) -> p h c r", h=2, c=BC)
        mhalf = views[4]

        ps0 = [ctx.enter_context(nc.psum_tensor(f"ps0_{j}", [P, 512], F32)) for j in range(BC)]
        ps1 = [ctx.enter_context(nc.psum_tensor(f"ps1_{j}", [P, 512], F32)) for j in range(BC)]
        psn = ctx.enter_context(nc.psum_tensor("psn", [P, 512], F32))

        WL = K1 * K1
        prep = xs[:, SLOTS - 1].rearrange("p c i w -> p (c i w)")
        at = [0]

        def scratch(n, dt=F32):
            words = n if dt == F32 else (n + 1) // 2
            v = prep[0:PC, at[0]:at[0] + words]
            at[0] += words
            return v if dt == F32 else v.bitcast(dt)

        p_wl = scratch(KC * WL).rearrange("p (k n) -> p k n", k=KC)
        p_ws = scratch(KC * 9).rearrange("p (k n) -> p k n", k=KC)
        p_k0 = scratch(KC * 9).rearrange("p (k n) -> p k n", k=KC)
        p_par = scratch(12 * KC).rearrange("p (b r k) -> p b r k", b=3, r=4)
        p_bn = scratch(4 * 3 * KC).rearrange("p (r b k) -> p r b k", r=4, b=3)
        p_sm = scratch(16 * KC).rearrange("p (r k) -> p r k", k=KC)
        p_w = scratch(KC * WL).rearrange("p (k n) -> p k n", k=KC)
        p_lo = scratch(KC * WL).rearrange("p (k n) -> p k n", k=KC)
        p_pad = [scratch(KC * K1 * PADT + 1, F16)[:, 0:KC * K1 * PADT] for _ in range(2)]
        p_pad = [v.rearrange("p (k d c) -> p k d c", k=KC, d=K1) for v in p_pad]
        T1N = BW * K1 * BW * 2 * WIN
        THN = HC * K1 * BW * 2
        T0N = K0 * 2 * K0
        p_zero = prep[:, at[0]:at[0] + R1N // 2].bitcast(F16)
        at[0] += R1N // 2
        p_t1 = blk[0:PC].rearrange("p r k a n u -> p (r k a n u)")[:, 0:KC * T1N].rearrange("p (k n) -> p k n", k=KC)
        p_th = scratch(KC * THN, F16).rearrange("p (k n) -> p k n", k=KC)
        p_t0 = scratch(KC * T0N, F16).rearrange("p (k n) -> p k n", k=KC)
        p_sc = scratch(3 * KC).rearrange("p (k r) -> p k r", r=3)
        assert at[0] <= GC * UI * P

        s_par = sem("params_loaded")
        s_prep = sem("prep_step")
        s_veps = sem("prep_var_ready")
        s_rstd = sem("prep_rstd_ready")
        s_tab = sem("tables_stored")
        s_scl = sem("scales_loaded")
        s_zero = sem("buffers_zeroed")
        s_exp = sem("exponent_written")
        s_held = sem("waits_held")
        s_ld = [sem(f"x_loaded_{j}") for j in range(BC)]
        s_w0 = sem("w0_loaded")
        s_w1 = [sem(f"w1_loaded_{r}") for r in range(Q)]
        s_m0 = [sem(f"matrices0_laid_{r}") for r in range(2)]
        s_m1 = [sem(f"matrices1_laid_{r}") for r in range(Q)]
        s_c0 = [sem(f"conv0_done_{j}") for j in range(BC)]
        s_c1 = [sem(f"conv1_done_{j}") for j in range(BC)]
        s_g0, s_h0, s_l0 = sem("norm0_done"), sem("high0_done"), sem("low0_done")
        s_g1, s_h1, s_l1 = sem("norm1_done"), sem("high1_done"), sem("low1_done")
        s_x1 = sem("layer0_summed")
        s_b1 = sem("stats1_taken")
        s_b0 = sem("stats0_taken")
        s_sc0, s_sc1 = sem("scales0_copied"), sem("scales1_copied")
        s_rg = [sem(f"regrouped_{r}") for r in range(2)]
        s_hl = [sem(f"halo_ready_{r}") for r in range(2)]
        s_ev = sem("sums_evacuated")
        s_yr = sem("sums_regrouped")
        s_fin = sem("layer1_summed")
        s_st = sem("stored")
        names = ["aggregated", "mean_summed", "mean_off", "mean_off_squared", "var_part", "var_summed",
                 "var_copied", "rstd_powered", "norm_scale", "norm_shift"]
        s_n = [{n: sem(f"{n}_{k}") for n in names} for k in range(2)]
        N_TAB = 16 * (4 + 2 * Q + 2)

        block = ctx.enter_context(nc.Block())

        def wait(eng, s, value):
            if not isinstance(value, int) or value > 0:
                eng.wait_ge(s, value)

        def hold(eng, s, value):
            wait(eng, s, value)
            if not isinstance(value, int):
                eng.sem_inc(s_held, 1)

        def schedule(eng, tick):
            for t in range(-2 * Q, 2 * Q):
                tick(Unit(0, t // Q), t % Q)
            with eng.Fori(1, NG - 1) as G:
                for t in range(2 * Q):
                    tick(Unit(G, t // Q), t % Q)
            for t in range((NU - 2) * Q, NT + L_FINAL):
                tick(Unit(0, t // Q), t % Q)

        def back(U, q, lag):
            return U + (q - lag) // Q, (q - lag) % Q

        def live(U):
            return not U.known or 0 <= U.number < NU

        def chan(U, q):
            return U.group_no * GC + q * BC

        def batch_no(U, q):
            return U.number * Q + q

        def slot(U):
            return xs[:, U.number % SLOTS]

        def ring(count_per, U, q):
            return (U.number * (Q // 2) + q // 2 + 1) * count_per

        def high_low(part, lo):
            v0 = 2 - lo
            return n1[:, 2 * lo:2 * lo + 2, part, :, v0:v0 + P // BW].rearrange("p j n v -> p n j v")

        @block.sync
        def _(sp):
            src = {"wl": (p_wl, w_large.rearrange("(k p) o a b -> p k (o a b)", p=PC)),
                   "ws": (p_ws, w_small.rearrange("(k p) o a b -> p k (o a b)", p=PC)),
                   "k0": (p_k0, k0.rearrange("(k p) o a b -> p k (o a b)", p=PC))}
            for dst, a in src.values():
                sp.dma_start(dst, a).then_inc(s_par, 16)
            with nc.allow_non_contiguous_dma(reason="one value per channel"):
                for b in range(3):
                    for r in range(4):
                        sp.dma_start(p_par[:, b, r, :],
                                     params[b][r].rearrange("(k p) -> p k", p=PC)).then_inc(s_par, 16)

            def load(U, q):
                V = U + 2
                if not live(V):
                    return
                b = batch_no(V, q)
                hold(sp, s_st, (b + 1 - SLOTS * Q) * BC * 16)
                if V.known and b == (SLOTS - 1) * Q:
                    sp.wait_ge(s_tab, N_TAB)
                for j in range(BC):
                    hold(sp, s_ld[j], b * 16)
                    sp.dma_start(slot(V)[:, q * BC + j],
                                 x[V.half * UI:(V.half + 1) * UI, chan(V, q) + j].rearrange("i h w -> h i w")
                                 ).then_inc(s_ld[j], 16)

            def regroup_sums(U, q):
                V, r = back(U, q, L_EVAC)
                if not live(V):
                    return
                b = batch_no(V, r)
                hold(sp, s_ev, b + 1)
                hold(sp, s_fin, b)
                p = ysum[:].ap[0][0]
                for k in range(NBLK):
                    sp.dma_start(yrow[BH * k:BH * (k + 1)].rearrange("p j n u -> p j (n u)"),
                                 ysum[:, k, :]).then_inc(s_yr, 16)

            def regroup_norm(U, q):
                V, r = back(U, q, L_NORM1)
                if not live(V):
                    return
                b = batch_no(V, r)
                if V.known and b == 0:
                    sp.wait_ge(s_tab, N_TAB)
                hold(sp, s_l1, b + 1)
                hold(sp, s_c1[BC - 1], b - 1)
                flat = n1[:].rearrange("p j a n u -> p j (a n u)")
                for k in range(NBLK):
                    sp.dma_start(blk[:, r % 2, k].rearrange("p a n u -> p (a n u)"), flat[BH * k:BH * (k + 1)])\
                        .then_inc(s_rg[r % 2], 16)

            def regroup_halo(U, q):
                V, r = back(U, q, L_HALO)
                if not live(V):
                    return
                hold(sp, s_rg[r % 2], ring(16 * NBLK, V, r))
                rows = blk[:, r % 2].rearrange("p k a n u -> p (k a n u)")
                n = (NBLK - 1) * RUN - (WIN - 1)
                for side in range(2):
                    p0 = (BH - R1) * BW if side == 0 else 0
                    src = rows[p0:p0 + R1 * BW, side * RUN:side * RUN + n]
                    sp.dma_start(halo[:, r % 2, side].rearrange("p k a n u -> p (k a n u)")[:, 0:n],
                                 bass.AP(tensor=src.tensor, offset=src.offset, ap=[src.ap[0], [1, WIN], [1, n]])
                                 ).then_inc(s_hl[r % 2], 16)

            def store(U, q):
                V, r = back(U, q, L_FINAL)
                if not live(V):
                    return
                hold(sp, s_fin, batch_no(V, r) + 1)
                for j in range(BC):
                    sp.dma_start(out[V.half * UI:(V.half + 1) * UI, chan(V, r) + j].rearrange("i h w -> h i w"),
                                 slot(V)[:, r * BC + j]).then_inc(s_st, 16)

            sp.wait_ge(s_zero, 1)

            def tick(U, q):
                regroup_halo(U, q)
                load(U, q)
                regroup_sums(U, q)
                store(U, q)
                regroup_norm(U, q)

            schedule(sp, tick)
            sp.wait_ge(s_st, NT * BC * 16)

        @block.gpsimd
        def _(pool):
            def load_scales(V):
                src = tabs[bass.ds(V.group_no * GC, GC)].rearrange("(o c) r -> o (c r)", o=1)
                pool.dma_start(scales[:, V.group_no % 2], src.to_broadcast([P, GC * 3])).then_inc(s_scl, 16)

            nc.gpsimd.memset(mhalf, -0.5).then_inc(s_exp, 1)
            pool.wait_ge(s_exp, 1)
            pool.wait_ge(s_veps, 1)
            for b in range(3):
                nc.gpsimd.tensor_tensor(p_bn[:, 1, b], p_bn[:, 0, b], mhalf[0:PC, 0:KC], ALU.pow).then_inc(s_rstd, 1)
            pool.wait_ge(s_prep, PREP_STEPS)
            kp = "(k p) n -> p k n"
            for t, v in ((tab1, p_t1), (tabh, p_th), (tab0, p_t0), (tabs, p_sc)):
                pool.dma_start(t.rearrange(kp, p=PC), v).then_inc(s_tab, 16)
            for t in (mat1, math, mat0):
                for r in range(t.shape[0]):
                    v = t[r].rearrange("c (s p) n -> p (c s) n", p=KH if t is math else P)
                    n, runs, width = v.shape
                    pool.dma_start(v, p_zero[0:n, 0:width].unsqueeze(1).to_broadcast([n, runs, width])).then_inc(s_tab, 16)
            pool.wait_ge(s_tab, N_TAB)
            load_scales(Unit(0, 0))

            def spread_bands(mat, r, c, tab, channel, first, cols, rows, step, done):
                row = mat.shape[3]
                run = tab.shape[1] // cols
                dst, src = mat[r, c], tab[bass.ds(channel, 1)]
                pool.dma_start(bass.AP(tensor=dst.tensor, offset=dst.offset + first,
                                       ap=[[row, cols], [cols * row + step, rows], [1, run]]),
                               bass.AP(tensor=src.tensor, offset=src.offset, ap=[[run, cols], [0, rows], [1, run]])
                               ).then_inc(done, 16)

            def lay0(U, q):
                V, r = back(U, q, -2)
                if not live(V):
                    return
                hold(pool, s_w0, (batch_no(V, r) - 1) * 16)
                src, dst = tab0[bass.ds(chan(V, r), BC)], mat0[r % 2]
                pool.dma_start(bass.AP(tensor=dst.tensor, offset=dst.offset,
                                       ap=[[P * R0N, BC], [R0N + 2 * K0, P], [1, T0N]]),
                               bass.AP(tensor=src.tensor, offset=src.offset, ap=[[T0N, BC], [0, P], [1, T0N]])
                               ).then_inc(s_m0[r % 2], 16)

            def load_w0(U, q):
                V, r = back(U, q, -1)
                if not live(V):
                    return
                b = batch_no(V, r)
                hold(pool, s_m0[r % 2], ring(16, V, r))
                hold(pool, s_c0[BC - 1], b)
                pool.dma_start(w0[:], mat0[r % 2, :, :, 2 * K0:2 * K0 + W0N].rearrange("c p n -> p c n"))\
                    .then_inc(s_w0, 16)

            def lay1(U, q):
                V, r = back(U, q, L_CONV1 - 3 - LAY_AHEAD)
                if not live(V):
                    return
                k = V.half * Q + r
                for c in range((BC * k + 1) // 2, (BC * (k + 1) + 1) // 2):
                    b, j = c // BC, c % BC
                    if j == 0:
                        hold(pool, s_w1[b], V.group_no * 32)
                    channel = V.group_no * GC + c
                    spread_bands(mat1, b, j, tab1, channel, 0, BW, BH, BW * 2 * WIN, s_m1[b])
                    for side in range(2):
                        first = side * (KH * RHN + (BH + R1) * BW * 2)
                        spread_bands(math, b, j, tabh, channel, first, HC, R1, BW * 2, s_m1[b])

            def load_w1(U, q):
                V, r = back(U, q, L_CONV1 - 3)
                if not live(V) or V.half:
                    return
                hold(pool, s_m1[r], (V.group_no + 1) * 16 * 3 * BC)
                hold(pool, s_c1[BC - 1], batch_no(V, r) - Q + 1)
                at1, ath = R1 * BW * 2 * WIN, 2 * R1 * BW * 2
                c = r * BC
                pool.dma_start(wblk[:, c:c + BC], mat1[r, :, :, at1:at1 + WSN].rearrange("c p n -> p c n"))\
                    .then_inc(s_w1[r], 16)
                pool.dma_start(whalo[:, c:c + BC].rearrange("p c s n -> p (c s) n"),
                               math[r, :, :, ath:ath + WHN].rearrange("c (s p) n -> p (c s) n", p=KH))\
                    .then_inc(s_w1[r], 16)

            def power(U, q, k):
                V = U + 1 if k == 0 else U
                if q != (2 if k == 0 else 3) or not live(V):
                    return
                pool.wait_ge(s_n[k]["var_copied"], V.number + 1)
                nc.gpsimd.tensor_tensor(nrm[k][:, 2], nrm[k][:, 3], mhalf[:, 0:UI], ALU.pow)\
                    .then_inc(s_n[k]["rstd_powered"], 1)

            def tick(U, q):
                load_w1(U, q)
                lay0(U, q)
                lay1(U, q)
                load_w0(U, q)
                power(U, q, 0)
                power(U, q, 1)
                if U.half == 1 and q == 2 and live(U) and live(U + 1):
                    hold(pool, s_sc1, (U + -1).number * Q)
                    load_scales(U + 1)

            schedule(pool, tick)

        @block.scalar
        def _(act):
            def evacuate(U, q):
                V, r = back(U, q, L_EVAC)
                if not live(V):
                    return
                b = batch_no(V, r)
                wait(act, s_yr, b * NBLK * 16)
                act.wait_ge(s_sc1, b + 1)
                for j in range(BC):
                    act.wait_ge(s_c1[j], b + 1)
                    ins = nc.scalar.activation(
                        ysum[:].rearrange("p k (c n) -> p k c n", c=BC)[:, :, j],
                        ps1[j][:].rearrange("p (k n) -> p k n", k=NBLK), ACT.Identity,
                        scale=sc1[:, r % 2, j, 0:1], bias=sc1[:, r % 2, j, 1:2])
                ins.then_inc(s_ev, 1)

            def norm(U, q, k, g):
                gv = g[:].rearrange("p (c i) w -> p c i w", c=BC)
                for i in range(UI):
                    ins = nc.scalar.activation(gv[:, :, i], slot(U)[:, q * BC:(q + 1) * BC, i], ACT.Identity,
                                               scale=nrm[k][:, 5, i:i + 1], bias=nrm[k][:, 6, i:i + 1])
                return ins

            def norm0(U, q):
                V, r = back(U, q, -1)
                if not live(V):
                    return
                b = batch_no(V, r)
                act.wait_ge(s_n[0]["norm_shift"], V.number + 1)
                hold(act, s_l0, b)
                norm(V, r, 0, g0).then_inc(s_g0, 1)
                act.wait_ge(s_g0, b + 1)
                wait(act, s_c0[BC - 1], b)
                nc.scalar.activation(n0[:, 0, :, 1:P + 1], g0[:], ACT.Copy).then_inc(s_h0, 1)

            def norm1(U, q):
                V, r = back(U, q, L_NORM1)
                if not live(V):
                    return
                b = batch_no(V, r)
                act.wait_ge(s_n[1]["norm_shift"], V.number + 1)
                hold(act, s_l1, b)
                norm(V, r, 1, g1).then_inc(s_g1, 1)
                act.wait_ge(s_g1, b + 1)
                if not V.known or b > 0:
                    pV, pr = back(V, r, 1)
                    act.wait_ge(s_rg[pr % 2], ring(16 * NBLK, pV, pr))
                gv = g1[:].rearrange("p n (v j) -> p n j v", j=BW)
                for lo in range(2):
                    ins = nc.scalar.activation(high_low(0, lo), gv[:, :, 2 - 2 * lo:4 - 2 * lo], ACT.Copy)
                ins.then_inc(s_h1, 1)

            act.wait_ge(s_zero, 1)

            def tick(U, q):
                evacuate(U, q)
                norm0(U, q)
                norm1(U, q)

            schedule(act, tick)

        @block.vector
        def _(dve):
            step = [0]

            def link(ins):
                ins.then_inc(s_prep, 1)
                step[0] += 1
                dve.wait_ge(s_prep, step[0])

            nc.vector.memset(n1[:], 0.0)
            nc.vector.memset(ones[:], 1.0 / P)
            nc.vector.memset(n0[:], 0.0).then_inc(s_zero, 1)
            dve.wait_ge(s_par, 15 * 16)
            nc.vector.tensor_scalar(p_bn[:, 0], p_par[:, :, 3], EPS, None, ALU.add).then_inc(s_veps, 1)
            dve.wait_ge(s_rstd, 3)
            link(nc.vector.tensor_tensor(p_bn[:, 2], p_par[:, :, 0], p_bn[:, 1], ALU.mult))
            link(nc.vector.tensor_tensor(p_bn[:, 3], p_par[:, :, 2], p_bn[:, 2], ALU.mult))
            link(nc.vector.tensor_tensor(p_bn[:, 3], p_par[:, :, 1], p_bn[:, 3], ALU.subtract))
            link(nc.vector.tensor_tensor(p_sm[:, 0], p_bn[:, 3, 0], p_bn[:, 3, 1], ALU.add))
            link(nc.vector.tensor_tensor(p_sc[:, :, 2], p_sm[:, 0], p_bn[:, 3, 2], ALU.add))

            def per_chunk(v, n):
                return v.unsqueeze(2).to_broadcast([PC, KC, n])

            link(nc.vector.tensor_tensor(p_w[:], p_wl[:], per_chunk(p_bn[:, 2, 0], WL), ALU.mult))
            link(nc.vector.tensor_tensor(p_ws[:], p_ws[:], per_chunk(p_bn[:, 2, 1], 9), ALU.mult))
            w2 = p_w.rearrange("p k (a b) -> p k a b", a=K1)
            c = K1 // 2
            link(nc.vector.tensor_tensor(w2[:, :, c - 1:c + 2, c - 1:c + 2], w2[:, :, c - 1:c + 2, c - 1:c + 2],
                                         p_ws.rearrange("p k (a b) -> p k a b", a=3), ALU.add))
            link(nc.vector.tensor_tensor(w2[:, :, c, c], w2[:, :, c, c], p_bn[:, 2, 2], ALU.add))

            def power_of_two(w, at_, s):
                mx, mn, pw, inv = (p_sm[:, at_ + i] for i in range(4))
                nc.vector.tensor_reduce(mx, w, AX.X, ALU.max)
                link(nc.vector.tensor_reduce(mn, w, AX.X, ALU.min))
                link(nc.vector.tensor_scalar(mn, mn, -1.0, 2.0 ** -100, ALU.mult, ALU.max))
                link(nc.vector.tensor_tensor(mx, mx, mn, ALU.max))
                link(nc.vector.tensor_scalar(pw.bitcast(U32), mx.bitcast(U32), 0x7F800000, None, ALU.bitwise_and))
                link(nc.vector.reciprocal(inv, pw))
                link(nc.vector.tensor_scalar(inv, inv, FILTER_SCALE, None, ALU.mult))
                link(nc.vector.tensor_scalar(s, pw, 1.0 / (FILTER_SCALE * NORM_SCALE), None, ALU.mult))
                return inv

            inv1 = power_of_two(p_w, 1, p_sc[:, :, 1])
            link(nc.vector.tensor_tensor(p_w[:], p_w[:], per_chunk(inv1, WL), ALU.mult))
            nc.vector.memset(p_pad[0], 0.0)
            nc.vector.memset(p_zero, 0.0)
            link(nc.vector.memset(p_pad[1], 0.0))
            pads = [v[:, :, :, BW - 1:BW - 1 + K1] for v in p_pad]
            link(nc.vector.tensor_copy(pads[0], w2))
            link(nc.vector.tensor_tensor(p_lo.rearrange("p k (a b) -> p k a b", a=K1), w2, pads[0], ALU.subtract))
            link(nc.vector.tensor_copy(pads[1], p_lo.rearrange("p k (a b) -> p k a b", a=K1)))
            t1 = p_t1.rearrange("p k (j d o a w) -> p k j d o a w", j=BW, d=K1, o=BW, a=2)
            th = p_th.rearrange("p k (j w d o a) -> p k j d o a w", j=BW, w=WIN, d=K1, o=BW)
            for tv in (t1, th):
                for j in range(BW):
                    for o in range(BW):
                        for a in range(2):
                            f = p_pad[a][:, :, K1 - 1, j - o + BW - 1:j - o + BW]
                            rev = bass.AP(tensor=f.tensor, offset=f.offset,
                                          ap=[f.ap[0], [K1 * PADT, KC], [-PADT, K1], [BW, WIN]])
                            ins = nc.vector.tensor_copy(tv[:, :, j, :, o, a, :], rev)
            link(ins)
            inv0 = power_of_two(p_k0, 6, p_sc[:, :, 0])
            link(nc.vector.tensor_tensor(p_k0[:], p_k0[:], per_chunk(inv0, 9), ALU.mult))
            t0 = p_t0.rearrange("p k (d a w) -> p k d a w", d=K0, a=2)
            for d in range(K0):
                ins = nc.vector.tensor_copy(t0[:, :, d, 0], p_k0[:, :, (K0 - 1 - d) * K0:(K0 - d) * K0])
            link(ins)
            for d in range(K0):
                ins = nc.vector.tensor_tensor(t0[:, :, d, 1], p_k0[:, :, (K0 - 1 - d) * K0:(K0 - d) * K0],
                                              t0[:, :, d, 0], ALU.subtract)
            link(ins)
            assert step[0] == PREP_STEPS, step[0]
            def final(U, q):
                V, r = back(U, q, L_FINAL)
                if not live(V):
                    return
                b = batch_no(V, r)
                dve.wait_ge(s_yr, (b + 1) * NBLK * 16)
                dve.wait_ge(s_x1, b + 1)
                xv = slot(V)[:, r * BC:(r + 1) * BC].rearrange("p c i (u j) -> p (c i) j u", j=BW)
                nc.vector.tensor_tensor(xv, xv, yrow[:].rearrange("p j n u -> p n j u"), ALU.add).then_inc(s_fin, 1)

            def copy_scales(U, q):
                def of_batch(V, r):
                    return scales[:, V.group_no % 2].rearrange("p (c r) -> p c r", r=3)[:, r * BC:(r + 1) * BC]

                if live(U):
                    if U.half == 0 and q == 0:
                        hold(dve, s_scl, (U.group_no + 1) * 16)
                    nc.vector.tensor_copy(sc0[:, q % 2], of_batch(U, q)[:, :, 0]).then_inc(s_sc0, 1)
                V, r = back(U, q, L_EVAC - 1)
                if live(V):
                    b = batch_no(V, r)
                    hold(dve, s_ev, b - 1)
                    nc.vector.tensor_copy(sc1[:, r % 2], of_batch(V, r)[:, :, 1:3]).then_inc(s_sc1, 1)

            def sum0(U, q):
                if not live(U):
                    return
                b = batch_no(U, q)
                dve.wait_ge(s_sc0, b + 1)
                for j in range(BC):
                    dve.wait_ge(s_c0[j], b + 1)
                    xv = slot(U)[:, q * BC + j].rearrange("p i w -> p (i w)")
                    ins = nc.vector.scalar_tensor_tensor(out=xv, in0=ps0[j][:], scalar=sc0[:, q % 2, j:j + 1],
                                                         in1=xv, op0=ALU.mult, op1=ALU.add)
                ins.then_inc(s_x1, 1)
                hold(dve, s_x1, b + 1)
                for i in range(UI):
                    ins = nc.vector.bn_stats(st[1][:, i, q], slot(U)[:, q * BC:(q + 1) * BC, i])
                ins.then_inc(s_b1, 1)

            def stats0(U, q):
                V, r = back(U, q, 1 - 2 * Q)
                if not live(V):
                    return
                b = batch_no(V, r)
                if r == 0:
                    hold(dve, s_n[0]["aggregated"], V.number)
                for j in range(BC):
                    hold(dve, s_ld[j], (b + 1) * 16)
                for i in range(UI):
                    ins = nc.vector.bn_stats(st[0][:, i, r], slot(V)[:, r * BC:(r + 1) * BC, i])
                ins.then_inc(s_b0, 1)
                if r == Q - 1:
                    hold(dve, s_b0, b + 1)
                    aggregate(0, V)

            def aggregate(k, V):
                mv = nrm[k][:, 0:2].rearrange("p a i -> p i a")
                for i in range(UI):
                    ins = nc.vector.bn_aggr(mv[:, i], st[k][:, i].rearrange("p a s -> p (a s)"))
                ins.then_inc(s_n[k]["aggregated"], 1)

            def finish_norm(k, V):
                s, n = s_n[k], nrm[k]
                dve.wait_ge(s["aggregated"], V.number + 1)
                dve.wait_ge(s["mean_summed"], V.number + 1)
                off = 8 * k
                nc.vector.tensor_copy(n[:, 7], psn[:, off:off + UI])
                nc.vector.tensor_tensor(n[:, 2], n[:, 0], psn[:, off:off + UI], ALU.subtract)\
                    .then_inc(s["mean_off"], 1)
                dve.wait_ge(s["mean_off"], V.number + 1)
                nc.vector.tensor_tensor(n[:, 3], n[:, 2], n[:, 2], ALU.mult).then_inc(s["mean_off_squared"], 1)
                dve.wait_ge(s["mean_off_squared"], V.number + 1)
                nc.vector.tensor_tensor(n[:, 4], n[:, 3], n[:, 1], ALU.add).then_inc(s["var_part"], 1)

            def finish_norm2(k, V):
                s, n = s_n[k], nrm[k]
                dve.wait_ge(s["var_summed"], V.number + 1)
                off = 8 * k + UI
                nc.vector.tensor_scalar(n[:, 3], psn[:, off:off + UI], EPS, None, ALU.add).then_inc(s["var_copied"], 1)

            def finish_norm3(k, V):
                s, n = s_n[k], nrm[k]
                dve.wait_ge(s["rstd_powered"], V.number + 1)
                wait(dve, s_g0 if k == 0 else s_g1, V.number * Q)
                nc.vector.tensor_scalar(n[:, 5], n[:, 2], NORM_SCALE, None, ALU.mult).then_inc(s["norm_scale"], 1)
                dve.wait_ge(s["norm_scale"], V.number + 1)
                nc.vector.scalar_tensor_tensor(out=n[:, 6], in0=n[:, 7], scalar=-1.0, in1=n[:, 5],
                                               op0=ALU.mult, op1=ALU.mult).then_inc(s["norm_shift"], 1)

            def low0(U, q):
                V, r = back(U, q, -1)
                if not live(V):
                    return
                dve.wait_ge(s_h0, batch_no(V, r) + 1)
                nc.vector.tensor_tensor(n0[:, 1, :, 1:P + 1], g0[:], n0[:, 0, :, 1:P + 1],
                                        ALU.subtract).then_inc(s_l0, 1)

            def low1(U, q):
                V, r = back(U, q, L_NORM1)
                if not live(V):
                    return
                dve.wait_ge(s_h1, batch_no(V, r) + 1)
                gv = g1[:].rearrange("p n (v j) -> p n j v", j=BW)
                for lo in range(2):
                    ins = nc.vector.tensor_tensor(high_low(1, lo), gv[:, :, 2 - 2 * lo:4 - 2 * lo],
                                                  high_low(0, lo), ALU.subtract)
                ins.then_inc(s_l1, 1)

            def tick(U, q):
                fin0 = q == 2 and live(U + 1)
                fin1 = q == 3 and live(U)
                copy_scales(U, q)
                if fin0:
                    finish_norm(0, U + 1)
                sum0(U, q)
                if fin0:
                    finish_norm2(0, U + 1)
                if fin1:
                    hold(dve, s_b1, batch_no(U, q) + 1)
                    aggregate(1, U)
                    finish_norm(1, U)
                low0(U, q)
                if fin0:
                    finish_norm3(0, U + 1)
                if fin1:
                    finish_norm2(1, U)
                final(U, q)
                if fin1:
                    finish_norm3(1, U)
                stats0(U, q)
                low1(U, q)

            schedule(dve, tick)

        @block.tensor
        def _(pe):
            def matrix(w, step, first):
                return w.rearrange("p (m n) -> p n m", n=step)[:, first]

            def conv0(U, q):
                if not live(U):
                    return
                b = batch_no(U, q)
                pe.wait_ge(s_w0, (b + 1) * 16)
                pe.wait_ge(s_l0, b + 1)
                wait(pe, s_x1, b)
                for j in range(BC):
                    n = 0
                    for wp, xp in PARTS:
                        for d in range(K0):
                            lhs = matrix(w0[:, j], 2 * K0, wp * K0 + d)
                            rhs = n0[:, xp, j * UI:(j + 1) * UI, d:d + P]
                            ins = nc.tensor.matmul(ps0[j][:].rearrange("p (i w) -> p i w", i=UI), lhs, rhs,
                                                   start=n == 0, stop=n == 3 * K0 - 1)
                            n += 1
                    ins.then_inc(s_c0[j], 1)

            def average(k, V, part):
                s = s_n[k]
                off = 8 * k + UI * part
                if part == 0:
                    pe.wait_ge(s["aggregated"], V.number + 1)
                    rhs, done = nrm[k][:, 0], s["mean_summed"]
                else:
                    pe.wait_ge(s["var_part"], V.number + 1)
                    rhs, done = nrm[k][:, 4], s["var_summed"]
                nc.tensor.matmul(psn[:, off:off + UI], ones[:], rhs, start=True, stop=True).then_inc(done, 1)

            def conv1_products(j, r):
                def main(wp, xp):
                    return [(matrix(wblk[:, r * BC + j], 2 * WIN, wp * WIN + a),
                             blk[:, r % 2, :, xp, j * UI:(j + 1) * UI, a:a + P // BW], 0, NBLK)
                            for a in range(WIN)]

                def sides(wp, xp):
                    return [(matrix(whalo[:, r * BC + j, side], 2, wp),
                             halo[:, r % 2, side, :, xp, j * UI:(j + 1) * UI, 0:P // BW], 1 - side, NBLK - side)
                            for side in range(2)]

                return main(*PARTS[0]) + [m for p in PARTS for m in sides(*p)] + main(*PARTS[1]) + main(*PARTS[2])

            def tick(U, q):
                V, r = back(U, q, L_CONV1)
                fin0 = q == 2 and live(U + 1)
                fin1 = q == 3 and live(U)
                if fin0:
                    average(0, U + 1, 0)
                conv0(U, q)
                if fin0:
                    average(0, U + 1, 1)
                if not live(V):
                    if fin1:
                        average(1, U, 0)
                        average(1, U, 1)
                    return
                b = batch_no(V, r)
                for j in range(BC):
                    if j == 0:
                        pe.wait_ge(s_w1[r], (V.group_no + 1) * 32)
                        pe.wait_ge(s_hl[r % 2], ring(16 * 2, V, r))
                        wait(pe, s_ev, b)
                    todo = conv1_products(j, r)
                    for n, (lhs, rhs, first, last) in enumerate(todo):
                        if fin1 and j == 1 and n in (0, 9):
                            average(1, U, n // 9)
                        ins = nc.tensor.matmul(ps1[j][:].rearrange("p (k i u) -> p k i u", k=NBLK, i=UI)[:, first:last], lhs, rhs,
                                               start=n == 0, stop=n == len(todo) - 1)
                    ins.then_inc(s_c1[j], 1)

            pe.wait_ge(s_zero, 1)
            schedule(pe, tick)


PREP_STEPS = 9 + 7 + 5 + 1 + 7 + 3

_PARAMS = [[f"L1_conv_{p}_{b}" for p in "gbmv"] for b in "lsi"]
_INS = ["x", "L0_conv_k", "L1_conv_w_large", "L1_conv_w_small"] + [n for row in _PARAMS for n in row]


def kernel(**inputs):
    import numpy as _np
    import concourse.bacc as _bacc
    from concourse import mybir as _mybir
    from concourse.bass_utils import run_bass_kernel_spmd as _run

    nc = _bacc.Bacc("TRN2", target_bir_lowering=False, num_devices=1)
    arrays, args = {}, {}
    for name in _INS:
        a = _np.ascontiguousarray(inputs[name])
        arrays[f"in_{name}_dram"] = a
        args[name] = nc.dram_tensor(f"in_{name}_dram", a.shape, _mybir.dt.from_np(a.dtype), kind="ExternalInput").ap()
    shape = inputs["x"].shape
    C = shape[1]
    out = nc.dram_tensor("out_0_dram", shape, _mybir.dt.float32, kind="ExternalOutput").ap()
    f16 = _mybir.dt.float16
    tab0 = nc.dram_tensor("tab0", (C, K0 * 2 * K0), f16, kind="Internal").ap()
    tab1 = nc.dram_tensor("tab1", (C, BW * K1 * BW * 2 * WIN), f16, kind="Internal").ap()
    tabh = nc.dram_tensor("tabh", (C, HC * K1 * BW * 2), f16, kind="Internal").ap()
    tabs = nc.dram_tensor("tabs", (C, 3), _mybir.dt.float32, kind="Internal").ap()
    mat0 = nc.dram_tensor("mat0", (2, BC, P, R0N), f16, kind="Internal").ap()
    mat1 = nc.dram_tensor("mat1", (Q, BC, P, R1N), f16, kind="Internal").ap()
    math = nc.dram_tensor("math", (Q, BC, 2 * KH, RHN), f16, kind="Internal").ap()
    preact_convs(nc, args["x"], args["L0_conv_k"], args["L1_conv_w_large"], args["L1_conv_w_small"],
                 [[args[n] for n in row] for row in _PARAMS], out, tab0, tab1, tabh, tabs, mat0, mat1, math)
    r = _run(nc, [arrays], core_ids=[0])
    return r.results[0]["out_0_dram"]
```

```python
from contextlib import ExitStack

import concourse.bass as bass
from concourse import mybir

F32 = mybir.dt.float32
F16 = mybir.dt.float16
U32 = mybir.dt.uint32
ALU = mybir.AluOpType
ACT = mybir.ActivationFunctionType
AX = mybir.AxisListType

P = 128
GC = 12
UI = 4
HALVES = 2
BC = 3
Q = GC // BC
SLOTS = 4
NBI = BC * UI
K0, K1 = 3, 13
R1 = K1 // 2
BW = 4
BH = P // BW
NBLK = P // BH
WIN = 4
HC = WIN * BW
KH = R1 * HC
UP = P // BW + WIN - 1
W0P = P + 2
RUN = 2 * NBI * UP
PADT = K1 - 1 + 2 * (BW - 1) + 1
NORM_SCALE = 128.0
FILTER_SCALE = 4096.0
EPS = 1e-5
PARTS = [(0, 0), (0, 1), (1, 0)]

R1N = (BH + 2 * R1) * BW * 2 * WIN
RHN = 3 * R1 * BW * 2
R0N = W0P * 2 * K0

L_CONV1 = 5
L_EVAC = 6
L_FINAL = 7
L_NORM1 = 3
L_HALO = 4
LAY_FIRST = 2 * Q
LAY_AHEAD = 5


class Unit:

    def __init__(self, group, n):
        self.group, self.n = group, n

    def __add__(self, k):
        return Unit(self.group, self.n + k)

    @property
    def known(self):
        return isinstance(self.group, int)

    @property
    def number(self):
        return self.group * HALVES + self.n

    @property
    def half(self):
        return self.n % HALVES

    @property
    def group_no(self):
        return self.group + self.n // HALVES


def preact_convs(nc, x, k0, w_large, w_small, params, out, tab0, tab1, tabh, tabs, mat0, mat1, math):
    N, C = x.shape[0], x.shape[1]
    NG = C // GC
    NU = NG * HALVES
    NT = NU * Q
    PC = min(P, C)
    KC = C // PC
    assert N == HALVES * UI and NG >= 3

    with ExitStack() as ctx:
        def sb(name, shape, dt):
            return ctx.enter_context(nc.sbuf_tensor(name, shape, dt))

        def sem(name):
            return ctx.enter_context(nc.semaphore(name))

        xs = sb("xs", [P, SLOTS, GC, UI, P], F32)
        g0 = sb("g0", [P, NBI, P], F32)
        g1 = sb("g1", [P, NBI, P], F32)
        n0 = sb("n0", [P, 2, NBI, W0P], F16)
        n1 = sb("n1", [P, BW, 2, NBI, UP], F16)
        blk = sb("blk", [P, 2, NBLK, 2, NBI, UP], F16)
        halo = sb("halo", [KH, 2, 2, NBLK - 1, 2, NBI, UP], F16)
        ysum = sb("ysum", [P, NBLK, NBI * (P // BW)], F32)
        yrow = sb("yrow", [P, BW, NBI, P // BW], F32)
        WSN = BH * BW * 2 * WIN
        wblk = sb("wblk", [P, GC, WSN], F16)
        WHN = BH * BW * 2
        whalo = sb("whalo", [KH, GC, 2, WHN], F16)
        W0N = P * 2 * K0
        w0 = sb("w0", [P, BC, W0N], F16)
        scales = sb("scales", [P, 2, GC * 3], F32)
        ones = sb("ones", [P, P], F32)
        st = [sb(f"st{k}", [P, UI, Q, 6], F32) for k in range(2)]
        NS = 8
        sizes = [NS * UI, NS * UI, 2 * BC, 2 * BC * 2, UI]
        small = sb("small", [P, sum(sizes)], F32)
        views = [small[:, sum(sizes[:i]):sum(sizes[:i + 1])] for i in range(len(sizes))]
        nrm = [v.rearrange("p (s i) -> p s i", s=NS) for v in views[0:2]]
        sc0 = views[2].rearrange("p (h c) -> p h c", h=2)
        sc1 = views[3].rearrange("p (h c r) -> p h c r", h=2, c=BC)
        mhalf = views[4]

        ps0 = [ctx.enter_context(nc.psum_tensor(f"ps0_{j}", [P, 512], F32)) for j in range(BC)]
        ps1 = [ctx.enter_context(nc.psum_tensor(f"ps1_{j}", [P, 512], F32)) for j in range(BC)]
        psn = ctx.enter_context(nc.psum_tensor("psn", [P, 512], F32))

        WL = K1 * K1
        prep = xs[:, SLOTS - 1].rearrange("p c i w -> p (c i w)")
        at = [0]

        def scratch(n, dt=F32):
            words = n if dt == F32 else (n + 1) // 2
            v = prep[0:PC, at[0]:at[0] + words]
            at[0] += words
            return v if dt == F32 else v.bitcast(dt)

        p_wl = scratch(KC * WL).rearrange("p (k n) -> p k n", k=KC)
        p_ws = scratch(KC * 9).rearrange("p (k n) -> p k n", k=KC)
        p_k0 = scratch(KC * 9).rearrange("p (k n) -> p k n", k=KC)
        p_par = scratch(12 * KC).rearrange("p (b r k) -> p b r k", b=3, r=4)
        p_bn = scratch(4 * 3 * KC).rearrange("p (r b k) -> p r b k", r=4, b=3)
        p_sm = scratch(16 * KC).rearrange("p (r k) -> p r k", k=KC)
        p_w = scratch(KC * WL).rearrange("p (k n) -> p k n", k=KC)
        p_lo = scratch(KC * WL).rearrange("p (k n) -> p k n", k=KC)
        p_pad = [scratch(KC * K1 * PADT + 1, F16)[:, 0:KC * K1 * PADT] for _ in range(2)]
        p_pad = [v.rearrange("p (k d c) -> p k d c", k=KC, d=K1) for v in p_pad]
        T1N = BW * K1 * BW * 2 * WIN
        THN = HC * K1 * BW * 2
        T0N = K0 * 2 * K0
        p_zero = prep[:, at[0]:at[0] + R1N // 2].bitcast(F16)
        at[0] += R1N // 2
        p_t1 = blk[0:PC].rearrange("p r k a n u -> p (r k a n u)")[:, 0:KC * T1N].rearrange("p (k n) -> p k n", k=KC)
        p_th = scratch(KC * THN, F16).rearrange("p (k n) -> p k n", k=KC)
        p_t0 = scratch(KC * T0N, F16).rearrange("p (k n) -> p k n", k=KC)
        p_sc = scratch(3 * KC).rearrange("p (k r) -> p k r", r=3)
        assert at[0] <= GC * UI * P

        s_par = sem("params_loaded")
        s_prep = sem("prep_step")
        s_veps = sem("prep_var_ready")
        s_rstd = sem("prep_rstd_ready")
        s_k0 = sem("k0_loaded")
        s_tab0 = sem("table0_stored")
        s_tab = sem("tables_stored")
        s_pz = sem("zeros_written")
        s_wz = sem("halo_filters_zeroed")
        s_clean0 = sem("matrices0_cleared")
        s_clean1 = sem("matrices1_cleared")
        s_scl = sem("scales_loaded")
        s_zero = sem("buffers_zeroed")
        s_exp = sem("exponent_written")
        s_held = sem("waits_held")
        s_ld = [sem(f"x_loaded_{j}") for j in range(BC)]
        s_w0 = sem("w0_loaded")
        s_w1 = [sem(f"w1_loaded_{r}") for r in range(Q)]
        s_m0 = [sem(f"matrices0_laid_{r}") for r in range(2)]
        s_m1 = [sem(f"matrices1_laid_{r}") for r in range(Q)]
        s_m1_first = [sem(f"first_matrices1_laid_{r}") for r in range(Q)]
        s_c0 = [sem(f"conv0_done_{j}") for j in range(BC)]
        s_c1 = [sem(f"conv1_done_{j}") for j in range(BC)]
        s_g0, s_h0, s_l0 = sem("norm0_done"), sem("high0_done"), sem("low0_done")
        s_g1, s_h1, s_l1 = sem("norm1_done"), sem("high1_done"), sem("low1_done")
        s_x1 = sem("layer0_summed")
        s_b1 = sem("stats1_taken")
        s_b0 = sem("stats0_taken")
        s_sc0, s_sc1 = sem("scales0_copied"), sem("scales1_copied")
        s_rg = [sem(f"regrouped_{r}") for r in range(2)]
        s_hl = [sem(f"halo_ready_{r}") for r in range(2)]
        s_ev = sem("sums_evacuated")
        s_yr = sem("sums_regrouped")
        s_fin = sem("layer1_summed")
        s_st = sem("stored")
        names = ["aggregated", "mean_summed", "mean_off", "mean_off_squared", "var_part", "var_summed",
                 "var_copied", "rstd_powered", "norm_scale", "norm_shift"]
        s_n = [{n: sem(f"{n}_{k}") for n in names} for k in range(2)]
        N_TAB = 16 * 3

        block = ctx.enter_context(nc.Block())

        def wait(eng, s, value):
            if not isinstance(value, int) or value > 0:
                eng.wait_ge(s, value)

        def hold(eng, s, value):
            wait(eng, s, value)
            if not isinstance(value, int):
                eng.sem_inc(s_held, 1)

        def schedule(eng, tick):
            for t in range(-2 * Q, 2 * Q):
                tick(Unit(0, t // Q), t % Q)
            with eng.Fori(1, NG - 1) as G:
                for t in range(2 * Q):
                    tick(Unit(G, t // Q), t % Q)
            for t in range((NU - 2) * Q, NT + L_FINAL):
                tick(Unit(0, t // Q), t % Q)

        def back(U, q, lag):
            return U + (q - lag) // Q, (q - lag) % Q

        def live(U):
            return not U.known or 0 <= U.number < NU

        def chan(U, q):
            return U.group_no * GC + q * BC

        def batch_no(U, q):
            return U.number * Q + q

        def norm_tick(k, U, q):
            if k == 1:
                return q == 3 and live(U)
            return q == (1 if U.known and U.number == -1 else 2) and live(U + 1)

        def slot(U):
            return xs[:, U.number % SLOTS]

        def lay_channel(eng, V, c):
            b, j = c // BC, c % BC
            done = s_m1_first[b] if V.known and V.group_no == 0 else s_m1[b]

            def spread(mat, tab, first, cols, rows, step):
                row, run = mat.shape[3], tab.shape[1] // cols
                dst, src = mat[b, j], tab[bass.ds(V.group_no * GC + c, 1)]
                eng.dma_start(bass.AP(tensor=dst.tensor, offset=dst.offset + first,
                                      ap=[[row, cols], [cols * row + step, rows], [1, run]]),
                              bass.AP(tensor=src.tensor, offset=src.offset, ap=[[run, cols], [0, rows], [1, run]])
                              ).then_inc(done, 16)

            spread(mat1, tab1, 0, BW, BH, BW * 2 * WIN)
            for side in range(2):
                spread(math, tabh, side * KH * RHN, HC, R1, BW * 2)

        def ring(count_per, U, q):
            return (U.number * (Q // 2) + q // 2 + 1) * count_per

        def high_low(part, lo):
            v0 = 2 - lo
            return n1[:, 2 * lo:2 * lo + 2, part, :, v0:v0 + P // BW].rearrange("p j n v -> p n j v")

        @block.sync
        def _(sp):
            sp.dma_start(p_k0, k0.rearrange("(k p) o a b -> p k (o a b)", p=PC)).then_inc(s_k0, 16)
            sp.dma_start(p_wl, w_large.rearrange("(k p) o a b -> p k (o a b)", p=PC)).then_inc(s_par, 16)
            sp.dma_start(p_ws, w_small.rearrange("(k p) o a b -> p k (o a b)", p=PC)).then_inc(s_par, 16)
            with nc.allow_non_contiguous_dma(reason="one value per channel"):
                for b in range(3):
                    for r in range(4):
                        sp.dma_start(p_par[:, b, r, :],
                                     params[b][r].rearrange("(k p) -> p k", p=PC)).then_inc(s_par, 16)

            def load(U, q):
                V = U + 2
                if not live(V):
                    return
                b = batch_no(V, q)
                if V.known and b == LAY_FIRST:
                    sp.wait_ge(s_tab, N_TAB)
                    sp.wait_ge(s_clean1, 16 * 2 * Q)
                    for c in range(GC):
                        lay_channel(sp, Unit(0, 0), c)
                hold(sp, s_st, (b + 1 - SLOTS * Q) * BC * 16)
                if V.known and b == Q:
                    sp.wait_ge(s_tab, N_TAB)
                if V.known and b == (SLOTS - 1) * Q:
                    sp.wait_ge(s_tab0, 16)
                    sp.wait_ge(s_clean0, 16 * 2)
                for j in range(BC):
                    hold(sp, s_ld[j], b * 16)
                    sp.dma_start(slot(V)[:, q * BC + j],
                                 x[V.half * UI:(V.half + 1) * UI, chan(V, q) + j].rearrange("i h w -> h i w")
                                 ).then_inc(s_ld[j], 16)

            def regroup_sums(U, q):
                V, r = back(U, q, L_EVAC)
                if not live(V):
                    return
                b = batch_no(V, r)
                hold(sp, s_ev, b + 1)
                hold(sp, s_fin, b)
                for k in range(NBLK):
                    sp.dma_start(yrow[BH * k:BH * (k + 1)].rearrange("p j n u -> p j (n u)"),
                                 ysum[:, k, :]).then_inc(s_yr, 16)

            def regroup_norm(U, q):
                V, r = back(U, q, L_NORM1)
                if not live(V):
                    return
                b = batch_no(V, r)
                if V.known and b == 0:
                    sp.wait_ge(s_tab, N_TAB)
                hold(sp, s_l1, b + 1)
                hold(sp, s_c1[BC - 1], b - 1)
                flat = n1[:].rearrange("p j a n u -> p j (a n u)")
                for k in range(NBLK):
                    sp.dma_start(blk[:, r % 2, k].rearrange("p a n u -> p (a n u)"), flat[BH * k:BH * (k + 1)])\
                        .then_inc(s_rg[r % 2], 16)

            def regroup_halo(U, q):
                V, r = back(U, q, L_HALO)
                if not live(V):
                    return
                hold(sp, s_rg[r % 2], ring(16 * NBLK, V, r))
                rows = blk[:, r % 2].rearrange("p k a n u -> p (k a n u)")
                n = (NBLK - 1) * RUN - (WIN - 1)
                for side in range(2):
                    p0 = (BH - R1) * BW if side == 0 else 0
                    src = rows[p0:p0 + R1 * BW, side * RUN:side * RUN + n]
                    sp.dma_start(halo[:, r % 2, side].rearrange("p k a n u -> p (k a n u)")[:, 0:n],
                                 bass.AP(tensor=src.tensor, offset=src.offset, ap=[src.ap[0], [1, WIN], [1, n]])
                                 ).then_inc(s_hl[r % 2], 16)

            def store(U, q):
                V, r = back(U, q, L_FINAL)
                if not live(V):
                    return
                hold(sp, s_fin, batch_no(V, r) + 1)
                for j in range(BC):
                    sp.dma_start(out[V.half * UI:(V.half + 1) * UI, chan(V, r) + j].rearrange("i h w -> h i w"),
                                 slot(V)[:, r * BC + j]).then_inc(s_st, 16)

            sp.wait_ge(s_zero, 1)

            def tick(U, q):
                regroup_halo(U, q)
                load(U, q)
                regroup_sums(U, q)
                store(U, q)
                regroup_norm(U, q)

            schedule(sp, tick)
            sp.wait_ge(s_st, NT * BC * 16)

        @block.gpsimd
        def _(pool):
            def load_scales(V):
                src = tabs[bass.ds(V.group_no * GC, GC)].rearrange("(o c) r -> o (c r)", o=1)
                pool.dma_start(scales[:, V.group_no % 2], src.to_broadcast([P, GC * 3])).then_inc(s_scl, 16)

            def clear(t, done):
                for r in range(t.shape[0]):
                    v = t[r].rearrange("c (s p) n -> p (c s) n", p=KH if t is math else P)
                    n, runs, width = v.shape
                    pool.dma_start(v, p_zero[0:n, 0:width].unsqueeze(1).to_broadcast([n, runs, width]))\
                        .then_inc(done, 16)

            def store_table(t, v, done):
                pool.dma_start(t.rearrange("(k p) n -> p k n", p=PC), v).then_inc(done, 16)

            def load_halves(dst, src, at, rows, reach, step, whole, done):
                for half in range(2):
                    first, last = (0, rows // 2 + reach) if half == 0 else (rows // 2 - reach, rows)
                    if whole:
                        first, last = 0, rows
                    ps = slice(half * P // 2, (half + 1) * P // 2)
                    pool.dma_start(dst[ps, :, first * step:last * step],
                                   src[:, ps, at + first * step:at + last * step].rearrange("c p n -> p c n"))\
                        .then_inc(done, 16)

            def lay0(U, q):
                V, r = back(U, q, -2)
                if not live(V):
                    return
                hold(pool, s_w0, (batch_no(V, r) - 1) * 32)
                src, dst = tab0[bass.ds(chan(V, r), BC)], mat0[r % 2]
                pool.dma_start(bass.AP(tensor=dst.tensor, offset=dst.offset,
                                       ap=[[P * R0N, BC], [R0N + 2 * K0, P], [1, T0N]]),
                               bass.AP(tensor=src.tensor, offset=src.offset, ap=[[T0N, BC], [0, P], [1, T0N]])
                               ).then_inc(s_m0[r % 2], 16)

            def load_w0(U, q):
                V, r = back(U, q, -1)
                if not live(V):
                    return
                b = batch_no(V, r)
                hold(pool, s_m0[r % 2], ring(16, V, r))
                hold(pool, s_c0[BC - 1], b)
                load_halves(w0[:], mat0[r % 2], 2 * K0, P, K0 // 2, 2 * K0, V.known and b == 0, s_w0)

            def lay1(U, q):
                V, r = back(U, q, L_CONV1 - 3 - LAY_AHEAD)
                if not live(V) or (V.known and V.group_no == 0):
                    return
                k = V.half * Q + r
                for c in range((BC * k + 1) // 2, (BC * (k + 1) + 1) // 2):
                    if c % BC == 0:
                        hold(pool, s_w1[c // BC], V.group_no * 64)
                    lay_channel(pool, V, c)

            def load_w1(U, q):
                V, r = back(U, q, L_CONV1 - 3)
                if not live(V) or V.half:
                    return
                if V.known and V.number == 0 and r == 0:
                    pool.wait_ge(s_wz, 1)
                if V.known and V.group_no == 0:
                    pool.wait_ge(s_m1_first[r], 16 * 3 * BC)
                else:
                    hold(pool, s_m1[r], V.group_no * 16 * 3 * BC)
                hold(pool, s_c1[BC - 1], batch_no(V, r) - Q + 1)
                cs = slice(r * BC, (r + 1) * BC)
                load_halves(wblk[:, cs], mat1[r], R1 * BW * 2 * WIN, BH, R1, BW * 2 * WIN,
                            V.known and V.group_no == 0, s_w1[r])
                n = R1 * BW * 2
                for side, at_row, out_row in ((0, 2 * R1, 0), (1, 0, BH - R1)):
                    src = math[r, :, side * KH:(side + 1) * KH, at_row * BW * 2:at_row * BW * 2 + n]
                    pool.dma_start(whalo[:, cs, side, out_row * BW * 2:out_row * BW * 2 + n],
                                   src.rearrange("c p n -> p c n")).then_inc(s_w1[r], 16)

            def power(U, q, k):
                V = U + 1 if k == 0 else U
                if not norm_tick(k, U, q):
                    return
                pool.wait_ge(s_n[k]["var_copied"], V.number + 1)
                nc.gpsimd.tensor_tensor(nrm[k][:, 2], nrm[k][:, 3], mhalf[:, 0:UI], ALU.pow)\
                    .then_inc(s_n[k]["rstd_powered"], 1)

            nc.gpsimd.memset(p_zero, 0.0).then_inc(s_pz, 1)
            nc.gpsimd.memset(mhalf, -0.5).then_inc(s_exp, 1)
            pool.wait_ge(s_pz, 1)
            clear(mat0, s_clean0)
            nc.gpsimd.memset(whalo[:].rearrange("p c s n -> p (c s n)").bitcast(F32), 0.0).then_inc(s_wz, 1)
            pool.wait_ge(s_prep, PREP0_STEPS)
            store_table(tab0, p_t0, s_tab0)
            pool.wait_ge(s_exp, 1)
            pool.wait_ge(s_veps, 1)
            for b in range(3):
                nc.gpsimd.tensor_tensor(p_bn[:, 1, b], p_bn[:, 0, b], mhalf[0:PC, 0:KC], ALU.pow).then_inc(s_rstd, 1)
            pool.wait_ge(s_tab0, 16)
            pool.wait_ge(s_clean0, 16 * 2)
            first = Unit(0, -1)
            lay0(first, Q - 2)
            lay0(first, Q - 1)
            load_w0(first, Q - 1)
            pool.wait_ge(s_prep, PREP_STEPS)
            for t, v in ((tab1, p_t1), (tabh, p_th), (tabs, p_sc)):
                store_table(t, v, s_tab)
            clear(mat1, s_clean1)
            clear(math, s_clean1)
            power(first, 1, 0)
            pool.wait_ge(s_tab, N_TAB)
            load_scales(Unit(0, 0))

            def tick(U, q):
                load_w1(U, q)
                ahead = U.known and U.number < 0
                if not ahead:
                    lay0(U, q)
                    load_w0(U, q)
                    power(U, q, 0)
                power(U, q, 1)
                lay1(U, q)
                if U.half == 1 and q == 2 and live(U) and live(U + 1):
                    hold(pool, s_sc1, U.group_no * HALVES * Q)
                    load_scales(U + 1)

            schedule(pool, tick)

        @block.scalar
        def _(act):
            def evacuate(U, q):
                V, r = back(U, q, L_EVAC)
                if not live(V):
                    return
                b = batch_no(V, r)
                wait(act, s_yr, b * NBLK * 16)
                act.wait_ge(s_sc1, b + 1)
                for j in range(BC):
                    act.wait_ge(s_c1[j], b + 1)
                    ins = nc.scalar.activation(
                        ysum[:].rearrange("p k (c n) -> p k c n", c=BC)[:, :, j],
                        ps1[j][:].rearrange("p (k n) -> p k n", k=NBLK), ACT.Identity,
                        scale=sc1[:, r % 2, j, 0:1], bias=sc1[:, r % 2, j, 1:2])
                ins.then_inc(s_ev, 1)

            def norm(U, q, k, g):
                gv = g[:].rearrange("p (c i) w -> p c i w", c=BC)
                for i in range(UI):
                    ins = nc.scalar.activation(gv[:, :, i], slot(U)[:, q * BC:(q + 1) * BC, i], ACT.Identity,
                                               scale=nrm[k][:, 5, i:i + 1], bias=nrm[k][:, 6, i:i + 1])
                return ins

            def norm0(U, q):
                V, r = back(U, q, -1)
                if not live(V):
                    return
                b = batch_no(V, r)
                act.wait_ge(s_n[0]["norm_shift"], V.number + 1)
                hold(act, s_l0, b)
                norm(V, r, 0, g0).then_inc(s_g0, 1)
                act.wait_ge(s_g0, b + 1)
                wait(act, s_c0[BC - 1], b)
                nc.scalar.activation(n0[:, 0, :, 1:P + 1], g0[:], ACT.Copy).then_inc(s_h0, 1)

            def norm1(U, q):
                V, r = back(U, q, L_NORM1)
                if not live(V):
                    return
                b = batch_no(V, r)
                act.wait_ge(s_n[1]["norm_shift"], V.number + 1)
                hold(act, s_l1, b)
                norm(V, r, 1, g1).then_inc(s_g1, 1)
                act.wait_ge(s_g1, b + 1)
                if not V.known or b > 0:
                    pV, pr = back(V, r, 1)
                    act.wait_ge(s_rg[pr % 2], ring(16 * NBLK, pV, pr))
                gv = g1[:].rearrange("p n (v j) -> p n j v", j=BW)
                for lo in range(2):
                    ins = nc.scalar.activation(high_low(0, lo), gv[:, :, 2 - 2 * lo:4 - 2 * lo], ACT.Copy)
                ins.then_inc(s_h1, 1)

            act.wait_ge(s_zero, 1)

            def tick(U, q):
                evacuate(U, q)
                norm0(U, q)
                norm1(U, q)

            schedule(act, tick)

        @block.vector
        def _(dve):
            step = [0]

            def link(ins):
                ins.then_inc(s_prep, 1)
                step[0] += 1
                dve.wait_ge(s_prep, step[0])

            def per_chunk(v, n):
                return v.unsqueeze(2).to_broadcast([PC, KC, n])

            def power_of_two(w, at_, s):
                mx, mn, pw, inv = (p_sm[:, at_ + i] for i in range(4))
                nc.vector.tensor_reduce(mx, w, AX.X, ALU.max)
                link(nc.vector.tensor_reduce(mn, w, AX.X, ALU.min))
                link(nc.vector.tensor_scalar(mn, mn, -1.0, 2.0 ** -100, ALU.mult, ALU.max))
                link(nc.vector.tensor_tensor(mx, mx, mn, ALU.max))
                link(nc.vector.tensor_scalar(pw.bitcast(U32), mx.bitcast(U32), 0x7F800000, None, ALU.bitwise_and))
                link(nc.vector.reciprocal(inv, pw))
                link(nc.vector.tensor_scalar(inv, inv, FILTER_SCALE, None, ALU.mult))
                link(nc.vector.tensor_scalar(s, pw, 1.0 / (FILTER_SCALE * NORM_SCALE), None, ALU.mult))
                return inv

            nc.vector.memset(ones[:], 1.0 / P)
            nc.vector.memset(n0[:], 0.0)
            dve.wait_ge(s_k0, 16)
            inv0 = power_of_two(p_k0, 6, p_sc[:, :, 0])
            link(nc.vector.tensor_tensor(p_k0[:], p_k0[:], per_chunk(inv0, 9), ALU.mult))
            t0 = p_t0.rearrange("p k (d a w) -> p k d a w", d=K0, a=2)
            for d in range(K0):
                ins = nc.vector.tensor_copy(t0[:, :, d, 0], p_k0[:, :, (K0 - 1 - d) * K0:(K0 - d) * K0])
            link(ins)
            for d in range(K0):
                ins = nc.vector.tensor_tensor(t0[:, :, d, 1], p_k0[:, :, (K0 - 1 - d) * K0:(K0 - d) * K0],
                                              t0[:, :, d, 0], ALU.subtract)
            link(ins)
            assert step[0] == PREP0_STEPS, step[0]
            nc.vector.memset(n1[:], 0.0).then_inc(s_zero, 1)
            dve.wait_ge(s_par, 14 * 16)
            nc.vector.tensor_scalar(p_bn[:, 0], p_par[:, :, 3], EPS, None, ALU.add).then_inc(s_veps, 1)
            dve.wait_ge(s_rstd, 3)
            link(nc.vector.tensor_tensor(p_bn[:, 2], p_par[:, :, 0], p_bn[:, 1], ALU.mult))
            link(nc.vector.tensor_tensor(p_bn[:, 3], p_par[:, :, 2], p_bn[:, 2], ALU.mult))
            link(nc.vector.tensor_tensor(p_bn[:, 3], p_par[:, :, 1], p_bn[:, 3], ALU.subtract))
            link(nc.vector.tensor_tensor(p_sm[:, 0], p_bn[:, 3, 0], p_bn[:, 3, 1], ALU.add))
            link(nc.vector.tensor_tensor(p_sc[:, :, 2], p_sm[:, 0], p_bn[:, 3, 2], ALU.add))

            link(nc.vector.tensor_tensor(p_w[:], p_wl[:], per_chunk(p_bn[:, 2, 0], WL), ALU.mult))
            link(nc.vector.tensor_tensor(p_ws[:], p_ws[:], per_chunk(p_bn[:, 2, 1], 9), ALU.mult))
            w2 = p_w.rearrange("p k (a b) -> p k a b", a=K1)
            c = K1 // 2
            link(nc.vector.tensor_tensor(w2[:, :, c - 1:c + 2, c - 1:c + 2], w2[:, :, c - 1:c + 2, c - 1:c + 2],
                                         p_ws.rearrange("p k (a b) -> p k a b", a=3), ALU.add))
            link(nc.vector.tensor_tensor(w2[:, :, c, c], w2[:, :, c, c], p_bn[:, 2, 2], ALU.add))

            inv1 = power_of_two(p_w, 1, p_sc[:, :, 1])
            link(nc.vector.tensor_tensor(p_w[:], p_w[:], per_chunk(inv1, WL), ALU.mult))
            nc.vector.memset(p_pad[0], 0.0)
            link(nc.vector.memset(p_pad[1], 0.0))
            pads = [v[:, :, :, BW - 1:BW - 1 + K1] for v in p_pad]
            link(nc.vector.tensor_copy(pads[0], w2))
            link(nc.vector.tensor_tensor(p_lo.rearrange("p k (a b) -> p k a b", a=K1), w2, pads[0], ALU.subtract))
            link(nc.vector.tensor_copy(pads[1], p_lo.rearrange("p k (a b) -> p k a b", a=K1)))
            t1 = p_t1.rearrange("p k (j d o a w) -> p k j d o a w", j=BW, d=K1, o=BW, a=2)
            th = p_th.rearrange("p k (j w d o a) -> p k j d o a w", j=BW, w=WIN, d=K1, o=BW)
            for tv in (t1, th):
                for j in range(BW):
                    for o in range(BW):
                        for a in range(2):
                            f = p_pad[a][:, :, K1 - 1, j - o + BW - 1:j - o + BW]
                            rev = bass.AP(tensor=f.tensor, offset=f.offset,
                                          ap=[f.ap[0], [K1 * PADT, KC], [-PADT, K1], [BW, WIN]])
                            ins = nc.vector.tensor_copy(tv[:, :, j, :, o, a, :], rev)
            link(ins)
            assert step[0] == PREP_STEPS, step[0]
            def final(U, q):
                V, r = back(U, q, L_FINAL)
                if not live(V):
                    return
                b = batch_no(V, r)
                dve.wait_ge(s_yr, (b + 1) * NBLK * 16)
                dve.wait_ge(s_x1, b + 1)
                xv = slot(V)[:, r * BC:(r + 1) * BC].rearrange("p c i (u j) -> p (c i) j u", j=BW)
                nc.vector.tensor_tensor(xv, xv, yrow[:].rearrange("p j n u -> p n j u"), ALU.add).then_inc(s_fin, 1)

            def copy_scales(U, q):
                def of_batch(V, r):
                    return scales[:, V.group_no % 2].rearrange("p (c r) -> p c r", r=3)[:, r * BC:(r + 1) * BC]

                if live(U):
                    if U.half == 0 and q == 0:
                        hold(dve, s_scl, (U.group_no + 1) * 16)
                    nc.vector.tensor_copy(sc0[:, q % 2], of_batch(U, q)[:, :, 0]).then_inc(s_sc0, 1)
                V, r = back(U, q, L_EVAC - 1)
                if live(V):
                    b = batch_no(V, r)
                    hold(dve, s_ev, b - 1)
                    nc.vector.tensor_copy(sc1[:, r % 2], of_batch(V, r)[:, :, 1:3]).then_inc(s_sc1, 1)

            def sum0(U, q):
                if not live(U):
                    return
                b = batch_no(U, q)
                dve.wait_ge(s_sc0, b + 1)
                for j in range(BC):
                    dve.wait_ge(s_c0[j], b + 1)
                    xv = slot(U)[:, q * BC + j].rearrange("p i w -> p (i w)")
                    ins = nc.vector.scalar_tensor_tensor(out=xv, in0=ps0[j][:], scalar=sc0[:, q % 2, j:j + 1],
                                                         in1=xv, op0=ALU.mult, op1=ALU.add)
                ins.then_inc(s_x1, 1)
                hold(dve, s_x1, b + 1)
                for i in range(UI):
                    ins = nc.vector.bn_stats(st[1][:, i, q], slot(U)[:, q * BC:(q + 1) * BC, i])
                ins.then_inc(s_b1, 1)

            def stats0(U, q):
                if U.known and U.number == 0 and q < 2:
                    batch_stats0(U + 1, 2 * q)
                    batch_stats0(U + 1, 2 * q + 1)
                V, r = back(U, q, 1 - 2 * Q)
                if not (V.known and V.number == 1):
                    batch_stats0(V, r)

            def batch_stats0(V, r):
                if not live(V):
                    return
                b = batch_no(V, r)
                if r == 0:
                    hold(dve, s_n[0]["aggregated"], V.number)
                for j in range(BC):
                    hold(dve, s_ld[j], (b + 1) * 16)
                for i in range(UI):
                    ins = nc.vector.bn_stats(st[0][:, i, r], slot(V)[:, r * BC:(r + 1) * BC, i])
                ins.then_inc(s_b0, 1)
                if r == Q - 1:
                    hold(dve, s_b0, b + 1)
                    aggregate(0, V)

            def aggregate(k, V):
                mv = nrm[k][:, 0:2].rearrange("p a i -> p i a")
                for i in range(UI):
                    ins = nc.vector.bn_aggr(mv[:, i], st[k][:, i].rearrange("p a s -> p (a s)"))
                ins.then_inc(s_n[k]["aggregated"], 1)

            def finish_norm(k, V):
                s, n = s_n[k], nrm[k]
                dve.wait_ge(s["aggregated"], V.number + 1)
                dve.wait_ge(s["mean_summed"], V.number + 1)
                off = 8 * k
                nc.vector.tensor_copy(n[:, 7], psn[:, off:off + UI])
                nc.vector.tensor_tensor(n[:, 2], n[:, 0], psn[:, off:off + UI], ALU.subtract)\
                    .then_inc(s["mean_off"], 1)
                dve.wait_ge(s["mean_off"], V.number + 1)
                nc.vector.tensor_tensor(n[:, 3], n[:, 2], n[:, 2], ALU.mult).then_inc(s["mean_off_squared"], 1)
                dve.wait_ge(s["mean_off_squared"], V.number + 1)
                nc.vector.tensor_tensor(n[:, 4], n[:, 3], n[:, 1], ALU.add).then_inc(s["var_part"], 1)

            def finish_norm2(k, V):
                s, n = s_n[k], nrm[k]
                dve.wait_ge(s["var_summed"], V.number + 1)
                off = 8 * k + UI
                nc.vector.tensor_scalar(n[:, 3], psn[:, off:off + UI], EPS, None, ALU.add).then_inc(s["var_copied"], 1)

            def finish_norm3(k, V):
                s, n = s_n[k], nrm[k]
                dve.wait_ge(s["rstd_powered"], V.number + 1)
                wait(dve, s_g0 if k == 0 else s_g1, V.number * Q)
                nc.vector.tensor_scalar(n[:, 5], n[:, 2], NORM_SCALE, None, ALU.mult).then_inc(s["norm_scale"], 1)
                dve.wait_ge(s["norm_scale"], V.number + 1)
                nc.vector.scalar_tensor_tensor(out=n[:, 6], in0=n[:, 7], scalar=-1.0, in1=n[:, 5],
                                               op0=ALU.mult, op1=ALU.mult).then_inc(s["norm_shift"], 1)

            def low0(U, q):
                V, r = back(U, q, -1)
                if not live(V):
                    return
                dve.wait_ge(s_h0, batch_no(V, r) + 1)
                nc.vector.tensor_tensor(n0[:, 1, :, 1:P + 1], g0[:], n0[:, 0, :, 1:P + 1],
                                        ALU.subtract).then_inc(s_l0, 1)

            def low1(U, q):
                V, r = back(U, q, L_NORM1)
                if not live(V):
                    return
                dve.wait_ge(s_h1, batch_no(V, r) + 1)
                gv = g1[:].rearrange("p n (v j) -> p n j v", j=BW)
                for lo in range(2):
                    ins = nc.vector.tensor_tensor(high_low(1, lo), gv[:, :, 2 - 2 * lo:4 - 2 * lo],
                                                  high_low(0, lo), ALU.subtract)
                ins.then_inc(s_l1, 1)

            def tick(U, q):
                fin0 = norm_tick(0, U, q)
                fin1 = norm_tick(1, U, q)
                copy_scales(U, q)
                if fin0:
                    finish_norm(0, U + 1)
                sum0(U, q)
                if fin0:
                    finish_norm2(0, U + 1)
                if fin1:
                    hold(dve, s_b1, batch_no(U, q) + 1)
                    aggregate(1, U)
                    finish_norm(1, U)
                low0(U, q)
                if fin0:
                    finish_norm3(0, U + 1)
                if fin1:
                    finish_norm2(1, U)
                final(U, q)
                if fin1:
                    finish_norm3(1, U)
                stats0(U, q)
                low1(U, q)

            schedule(dve, tick)

        @block.tensor
        def _(pe):
            def matrix(w, step, first):
                return w.rearrange("p (m n) -> p n m", n=step)[:, first]

            def conv0(U, q):
                if not live(U):
                    return
                b = batch_no(U, q)
                pe.wait_ge(s_w0, (b + 1) * 32)
                pe.wait_ge(s_l0, b + 1)
                wait(pe, s_x1, b)
                for j in range(BC):
                    middle, left, right = K0 // 2, 0, K0 - 1
                    order = [(p, d) for p in PARTS[:2] for d in (middle, left, right)]
                    order += [(PARTS[2], d) for d in (left, right, middle)]
                    for n, ((wp, xp), d) in enumerate(order):
                        c0, c1 = int(d == left), P - int(d == right)
                        lhs = matrix(w0[:, j], 2 * K0, wp * K0 + d)
                        rhs = n0[:, xp, j * UI:(j + 1) * UI, d + c0:d + c1]
                        ins = nc.tensor.matmul(ps0[j][:].rearrange("p (i w) -> p i w", i=UI)[:, :, c0:c1], lhs, rhs,
                                               start=n == 0, stop=n == len(order) - 1)
                    ins.then_inc(s_c0[j], 1)

            def average(k, V, part):
                s = s_n[k]
                off = 8 * k + UI * part
                if part == 0:
                    pe.wait_ge(s["aggregated"], V.number + 1)
                    rhs, done = nrm[k][:, 0], s["mean_summed"]
                else:
                    pe.wait_ge(s["var_part"], V.number + 1)
                    rhs, done = nrm[k][:, 4], s["var_summed"]
                nc.tensor.matmul(psn[:, off:off + UI], ones[:], rhs, start=True, stop=True).then_inc(done, 1)

            def conv1_products(j, r):
                UB = P // BW

                def main(wp, xp, windows):
                    todo = []
                    for a in windows:
                        u0, u1 = int(a == 0), UB - int(a == WIN - 1)
                        todo.append((matrix(wblk[:, r * BC + j], 2 * WIN, wp * WIN + a),
                                     blk[:, r % 2, :, xp, j * UI:(j + 1) * UI, u0 + a:u1 + a], (0, NBLK), (u0, u1)))
                    return todo

                def sides(wp, xp):
                    return [(matrix(whalo[:, r * BC + j, side], 2, wp),
                             halo[:, r % 2, side, :, xp, j * UI:(j + 1) * UI, 0:UB], (1 - side, NBLK - side), (0, UB))
                            for side in range(2)]

                inner_first, inner_last = (1, 0, 2, 3), (0, 1, 3, 2)
                return (main(*PARTS[0], inner_first) + [m for p in PARTS for m in sides(*p)]
                        + main(*PARTS[1], inner_first) + main(*PARTS[2], inner_last))

            def tick(U, q):
                V, r = back(U, q, L_CONV1)
                fin0 = norm_tick(0, U, q)
                fin1 = norm_tick(1, U, q)
                if fin0:
                    average(0, U + 1, 0)
                conv0(U, q)
                if fin0:
                    average(0, U + 1, 1)
                if not live(V):
                    if fin1:
                        average(1, U, 0)
                        average(1, U, 1)
                    return
                b = batch_no(V, r)
                for j in range(BC):
                    if j == 0:
                        pe.wait_ge(s_w1[r], (V.group_no + 1) * 64)
                        pe.wait_ge(s_hl[r % 2], ring(16 * 2, V, r))
                        wait(pe, s_ev, b)
                    todo = conv1_products(j, r)
                    sums = ps1[j][:].rearrange("p (k i u) -> p k i u", k=NBLK, i=UI)
                    for n, (lhs, rhs, ks, us) in enumerate(todo):
                        if fin1 and j == 1 and n in (3, 12):
                            average(1, U, n // 12)
                        ins = nc.tensor.matmul(sums[:, ks[0]:ks[1], :, us[0]:us[1]], lhs, rhs,
                                               start=n == 0, stop=n == len(todo) - 1)
                    ins.then_inc(s_c1[j], 1)

            pe.wait_ge(s_zero, 1)
            schedule(pe, tick)


PREP0_STEPS = 7 + 3
PREP_STEPS = PREP0_STEPS + 9 + 7 + 5 + 1

_PARAMS = [[f"L1_conv_{p}_{b}" for p in "gbmv"] for b in "lsi"]
_INS = ["x", "L0_conv_k", "L1_conv_w_large", "L1_conv_w_small"] + [n for row in _PARAMS for n in row]


def kernel(**inputs):
    import numpy as _np
    import concourse.bacc as _bacc
    from concourse import mybir as _mybir
    from concourse.bass_utils import run_bass_kernel_spmd as _run

    nc = _bacc.Bacc("TRN2", target_bir_lowering=False, num_devices=1)
    arrays, args = {}, {}
    for name in _INS:
        a = _np.ascontiguousarray(inputs[name])
        arrays[f"in_{name}_dram"] = a
        args[name] = nc.dram_tensor(f"in_{name}_dram", a.shape, _mybir.dt.from_np(a.dtype), kind="ExternalInput").ap()
    shape = inputs["x"].shape
    C = shape[1]
    out = nc.dram_tensor("out_0_dram", shape, _mybir.dt.float32, kind="ExternalOutput").ap()
    f16 = _mybir.dt.float16
    tab0 = nc.dram_tensor("tab0", (C, K0 * 2 * K0), f16, kind="Internal").ap()
    tab1 = nc.dram_tensor("tab1", (C, BW * K1 * BW * 2 * WIN), f16, kind="Internal").ap()
    tabh = nc.dram_tensor("tabh", (C, HC * K1 * BW * 2), f16, kind="Internal").ap()
    tabs = nc.dram_tensor("tabs", (C, 3), _mybir.dt.float32, kind="Internal").ap()
    mat0 = nc.dram_tensor("mat0", (2, BC, P, R0N), f16, kind="Internal").ap()
    mat1 = nc.dram_tensor("mat1", (Q, BC, P, R1N), f16, kind="Internal").ap()
    math = nc.dram_tensor("math", (Q, BC, 2 * KH, RHN), f16, kind="Internal").ap()
    preact_convs(nc, args["x"], args["L0_conv_k"], args["L1_conv_w_large"], args["L1_conv_w_small"],
                 [[args[n] for n in row] for row in _PARAMS], out, tab0, tab1, tabh, tabs, mat0, mat1, math)
    r = _run(nc, [arrays], core_ids=[0])
    return r.results[0]["out_0_dram"]
```
